# Optimizing a Trainium2 kernel written in Bass

```python
import numpy as np
import jax
import jax.numpy as jnp

def _softmax(x, axis=-1):
    return jax.nn.softmax(x, axis=axis)

def _gelu(x):
    return jax.nn.gelu(x, approximate=True)

def _silu(x):
    return jax.nn.silu(x)

def _sigmoid(x):
    return jax.nn.sigmoid(x)

def _layernorm(x, axis=-1, eps=1e-05):
    m = jnp.mean(x, axis=axis, keepdims=True)
    v = jnp.var(x, axis=axis, keepdims=True)
    return (x - m) / jnp.sqrt(v + eps)

def _scatter_add(tgt, idx, src, axis=0):
    return tgt.at[idx].add(src)

def _segment_sum(src, seg, n):
    return jax.ops.segment_sum(src, seg, n)
kernel_name = 'mk_perceiver_d1_seqx_r4_5efe26'

def setup_inputs(seed: int=0):
    np.random.seed(seed)
    _w = jnp.asarray

    def _rec_inputs():
        import jax
        import jax.numpy as jnp
        _rk = jax.random.key(seed)
        x = -0.000125 + 0.9999 * jax.random.normal(jax.random.fold_in(_rk, 1), (1, 256, 512), jnp.float32)
        _lenS = 256 - jax.random.randint(jax.random.fold_in(_rk, 7), (1,), 0, max(1, 256 // 4) + 1, jnp.int32)
        _lenS2 = 4096 - jax.random.randint(jax.random.fold_in(_rk, 8), (1,), 0, max(1, 4096 // 4) + 1, jnp.int32)
        _ctx_2048P = jax.random.normal(jax.random.fold_in(_rk, 11), (1, 16, 512), jnp.float32)
        _ctx_2048c = jax.random.dirichlet(jax.random.fold_in(_rk, 511), 0.3 * jnp.ones((16,), jnp.float32), (1, 4096))
        _ctx_2048t = jnp.einsum('bsk,bkd->bsd', _ctx_2048c, _ctx_2048P)
        _ctx_2048t = _ctx_2048t * jax.lax.rsqrt(jnp.mean(jnp.square(_ctx_2048t)) + 1e-12) * 0.953939
        ctx_2048 = -0.000514642 + 1.00011 * (_ctx_2048t + 0.3 * jax.random.normal(jax.random.fold_in(_rk, 611), (1, 4096, 512), jnp.float32))
        _validS = jnp.arange(256)[None, :] < _lenS[:, None]
        _validS2 = jnp.arange(4096)[None, :] < _lenS2[:, None]
        _causal = jnp.tril(jnp.ones((256, 256), dtype=bool))
        mask_BxS2_bk0 = jnp.logical_not(jnp.broadcast_to(_validS2[:, :], (1, 4096)))
        return (x, ctx_2048, mask_BxS2_bk0)
    x, ctx_2048, mask_BxS2_bk0 = _rec_inputs()

    def _L0_xattn_setup():
        import jax, jax.numpy as jnp
        import numpy as np
        key = jax.random.key(seed)
        k1, k2, k3 = jax.random.split(key, 3)
        B, S, D, M = (8, 512, 512, 128)
        hidden_states = jax.random.normal(k1, (B, S, D), dtype=jnp.float32)
        memory_tokens = jax.random.normal(k2, (B, M, D), dtype=jnp.float32)
        memory_mask = jax.random.randint(k3, (B, M), 0, 2).astype(jnp.bool_)
        return {'hidden_states': hidden_states, 'memory_tokens': memory_tokens, 'memory_mask': memory_mask}
    _L0_xattn_all = _L0_xattn_setup()
    _L0_xattn_in = {k: v for k, v in _L0_xattn_all.items() if k in ()}
    del _L0_xattn_all

    def _L0_attn_setup():
        import jax, jax.numpy as jnp
        import numpy as np
        NUM_HEADS = 16
        ROPE_BASE = 10000.0
        QK_GAIN_INIT = 12.0
        EPS = 1e-06
        ROPE_MASK = jnp.asarray(np.tile([1.0, 0.0], NUM_HEADS // 2), dtype=jnp.float32)

        def _rope_cos_sin(seqlen, head_dim, dtype):
            half = head_dim // 2
            inv_freq = ROPE_BASE ** (-jnp.arange(0, half, dtype=jnp.float32) / half)
            theta = jnp.arange(seqlen, dtype=jnp.float32)[:, None] * inv_freq[None, :]
            return (jnp.cos(theta).astype(dtype), jnp.sin(theta).astype(dtype))

        def _apply_rope(t, cos, sin):
            d2 = t.shape[-1] // 2
            t1, t2 = (t[..., :d2], t[..., d2:])
            c = cos[None, :, None, :]
            s = sin[None, :, None, :]
            return jnp.concatenate([t1 * c - t2 * s, t1 * s + t2 * c], axis=-1)

        def _unit_norm(t):
            return t * jax.lax.rsqrt(jnp.sum(t * t, axis=-1, keepdims=True) + EPS)
        key = jax.random.key(seed)
        k0, k1, k2 = jax.random.split(key, 3)
        B, S, Dm = (2, 512, 512)
        x = jax.random.normal(k0, (B, S, Dm), dtype=jnp.float32)
        w_qkv = jax.random.normal(k1, (Dm, 3 * Dm), dtype=jnp.float32) * Dm ** (-0.5)
        w_out = jax.random.normal(k2, (Dm, Dm), dtype=jnp.float32) * Dm ** (-0.5)
        q_gain = jnp.full((NUM_HEADS,), QK_GAIN_INIT, dtype=jnp.float32)
        return {'x': x, 'w_qkv': w_qkv, 'w_out': w_out, 'q_gain': q_gain}
    _L0_attn_all = _L0_attn_setup()
    _L0_attn_in = {k: v for k, v in _L0_attn_all.items() if k in ('w_qkv', 'w_out', 'q_gain')}
    del _L0_attn_all

    def _L0_ffn_setup():
        import jax, jax.numpy as jnp
        import numpy as np
        B, S, H, I, E, K = (2, 256, 512, 192, 64, 8)
        key = jax.random.key(seed)
        ks = jax.random.split(key, 5)
        lecun = lambda k, shape, fan_in: jax.random.normal(k, shape, jnp.float32) / np.sqrt(fan_in).astype(np.float32)
        return {'hidden_states': jax.random.normal(ks[0], (B, S, H), jnp.float32), 'gate_w': lecun(ks[1], (H, E), H), 'gate_proj_w': lecun(ks[2], (E, H, I), H), 'up_proj_w': lecun(ks[3], (E, H, I), H), 'down_proj_w': lecun(ks[4], (E, I, H), I)}
    _L0_ffn_all = _L0_ffn_setup()
    _L0_ffn_in = {k: v for k, v in _L0_ffn_all.items() if k in ('gate_w', 'gate_proj_w', 'up_proj_w', 'down_proj_w')}
    del _L0_ffn_all
    return {'x': x, 'ctx_2048': ctx_2048, 'mask_BxS2_bk0': mask_BxS2_bk0, 'L0_attn_w_qkv': _L0_attn_in['w_qkv'], 'L0_attn_w_out': _L0_attn_in['w_out'], 'L0_attn_q_gain': _L0_attn_in['q_gain'], 'L0_ffn_gate_w': _L0_ffn_in['gate_w'], 'L0_ffn_gate_proj_w': _L0_ffn_in['gate_proj_w'], 'L0_ffn_up_proj_w': _L0_ffn_in['up_proj_w'], 'L0_ffn_down_proj_w': _L0_ffn_in['down_proj_w']}

def reference(x, ctx_2048, mask_BxS2_bk0, L0_attn_w_qkv, L0_attn_w_out, L0_attn_q_gain, L0_ffn_gate_w, L0_ffn_gate_proj_w, L0_ffn_up_proj_w, L0_ffn_down_proj_w):
    import jax
    import jax.numpy as jnp

    def _L0_xattn_ref(hidden_states, memory_tokens, memory_mask):
        import jax, jax.numpy as jnp
        import numpy as np
        B, S, D = hidden_states.shape
        scale = 1.0 / jnp.sqrt(jnp.asarray(D, hidden_states.dtype))
        scores = jnp.einsum('bsd,bmd->bsm', hidden_states, memory_tokens) * scale
        neg_inf = jnp.asarray(-1e+30, scores.dtype)
        scores = jnp.where(memory_mask[:, None, :], scores, neg_inf)
        attn = jax.nn.softmax(scores, axis=-1)
        readout = jnp.einsum('bsm,bmd->bsd', attn, memory_tokens)
        valid_b = jnp.any(memory_mask, axis=-1)
        out = jnp.where(valid_b[:, None, None], readout, jnp.zeros_like(readout))
        return out

    def _L0_attn_ref(x, w_qkv, w_out, q_gain):
        import jax, jax.numpy as jnp
        import numpy as np
        NUM_HEADS = 16
        ROPE_BASE = 10000.0
        QK_GAIN_INIT = 12.0
        EPS = 1e-06
        ROPE_MASK = jnp.asarray(np.tile([1.0, 0.0], NUM_HEADS // 2), dtype=jnp.float32)

        def _rope_cos_sin(seqlen, head_dim, dtype):
            half = head_dim // 2
            inv_freq = ROPE_BASE ** (-jnp.arange(0, half, dtype=jnp.float32) / half)
            theta = jnp.arange(seqlen, dtype=jnp.float32)[:, None] * inv_freq[None, :]
            return (jnp.cos(theta).astype(dtype), jnp.sin(theta).astype(dtype))

        def _apply_rope(t, cos, sin):
            d2 = t.shape[-1] // 2
            t1, t2 = (t[..., :d2], t[..., d2:])
            c = cos[None, :, None, :]
            s = sin[None, :, None, :]
            return jnp.concatenate([t1 * c - t2 * s, t1 * s + t2 * c], axis=-1)

        def _unit_norm(t):
            return t * jax.lax.rsqrt(jnp.sum(t * t, axis=-1, keepdims=True) + EPS)
        B, S, Dm = x.shape
        H = NUM_HEADS
        D = Dm // H
        qkv = (x @ w_qkv).reshape(B, S, 3, H, D)
        q, k, v = (qkv[:, :, 0], qkv[:, :, 1], qkv[:, :, 2])
        q = _unit_norm(q)
        k = _unit_norm(k)
        cos, sin = _rope_cos_sin(S, D, x.dtype)
        m = ROPE_MASK[None, None, :, None]
        q = m * _apply_rope(q, cos, sin) + (1.0 - m) * q
        k = m * _apply_rope(k, cos, sin) + (1.0 - m) * k
        logits = jnp.einsum('bshd,bthd->bhst', q, k) * q_gain[None, :, None, None]
        causal = jnp.tril(jnp.ones((S, S), dtype=bool))
        logits = jnp.where(causal[None, None], logits, jnp.finfo(logits.dtype).min)
        attn = jax.nn.softmax(logits, axis=-1)
        y = jnp.einsum('bhst,bthd->bshd', attn, v).reshape(B, S, Dm)
        return y @ w_out

    def _L0_ffn_ref(hidden_states, gate_w, gate_proj_w, up_proj_w, down_proj_w):
        import jax, jax.numpy as jnp
        import numpy as np
        B, S, H, I, E, K = (2, 256, 512, 192, 64, 8)
        b, s, h = hidden_states.shape
        x = hidden_states.reshape(-1, h)
        router_logits = x @ gate_w
        routing_weights, selected = jax.lax.top_k(router_logits, K)
        routing_weights = jax.nn.softmax(routing_weights, axis=-1)
        flat_sel = selected.reshape(-1)
        order = jnp.argsort(flat_sel)
        hidden_sorted = jnp.repeat(x, K, axis=0)[order]
        group_sizes = jnp.zeros((E,), jnp.int32).at[flat_sel].add(1)
        gate = jax.lax.ragged_dot(hidden_sorted, gate_proj_w, group_sizes)
        up = jax.lax.ragged_dot(hidden_sorted, up_proj_w, group_sizes)
        down = jax.lax.ragged_dot(jax.nn.silu(gate) * up, down_proj_w, group_sizes)
        unsort = jnp.argsort(order)
        out = down[unsort].reshape(-1, K, h)
        out = jnp.sum(out * routing_weights[..., None], axis=1)
        return out.reshape(b, s, h)
    x = x + _L0_xattn_ref(_layernorm(x, axis=-1), ctx_2048, mask_BxS2_bk0)
    x = x + _L0_attn_ref(_layernorm(x, axis=-1), L0_attn_w_qkv, L0_attn_w_out, L0_attn_q_gain)
    x = x + _L0_ffn_ref(_layernorm(x, axis=-1), L0_ffn_gate_w, L0_ffn_gate_proj_w, L0_ffn_up_proj_w, L0_ffn_down_proj_w)
    return x

_drawn_inputs = setup_inputs


def setup_inputs(seed=0):
    import zlib

    import numpy as np

    out = dict(_drawn_inputs(seed))
    spreads = {'L0_attn_q_gain': (12.0, 0.2)}
    factors = {}
    for name, (base, spread) in spreads.items():
        noise = np.random.default_rng([zlib.crc32(name.encode()), seed]).standard_normal(out[name].shape)
        drawn = base * np.exp(spread * noise) if base else spread * noise
        out[name] = jnp.asarray(drawn.astype(out[name].dtype))
    for name, factor in factors.items():
        out[name] = (out[name] * factor).astype(out[name].dtype)
    return out
```

```python
import numpy as np
import concourse.bass as bass
from concourse import mybir
from contextlib import ExitStack

F32 = mybir.dt.float32
BF16 = mybir.dt.bfloat16
F16 = mybir.dt.float16
I32 = mybir.dt.int32
U8 = mybir.dt.uint8
ALU = mybir.AluOpType
ACT = mybir.ActivationFunctionType
AX = mybir.AxisListType

P = 128
TOK, D = 256, 512
TH = TOK // P
DC = D // P
MEM = 4096
GRP = 512
NG = MEM // GRP
KC = GRP // P
HEADS, HD = 16, 32
HG = 4
EXP_N, TOPK, INTER = 64, 8, 192
HALF_I = INTER // 2
PAIRS = EXP_N // 2
BLK = 64
RING = 4
LAPS = PAIRS // RING
EPS_LN, EPS_UNIT = 1e-5, 1e-6
XSCALE = float(1.0 / np.sqrt(np.float32(D)))
BIG = 1e30
LOWEST = -3.0e38


def perceiver(nc, x, ctxm, mask, w_qkv, w_out, q_gain, gate_w, gate_proj, up_proj, down_proj,
              rope_cs, out):
    es = ExitStack()
    with es:
        def sb(name, shape, dt=F32):
            return es.enter_context(nc.sbuf_tensor(name, shape, dt))

        def sem(name):
            return es.enter_context(nc.semaphore(name))

        psum = es.enter_context(nc.psum_tensor("psum", [P, 8, 512], F32))
        bank = [psum[:, i, :] for i in range(8)]

        ident = sb("ident", [P, P])
        ident_b = sb("ident_b", [P, P], BF16)
        causal_b = sb("causal_b", [P, 3, P], BF16)
        blk_c = sb("blk_c", [P, TH, 2])
        slot_row = sb("slot_row", [P, BLK])
        ones_b = sb("ones_b", [P, P], BF16)
        later_b = sb("later_b", [P, TH, TOK], BF16)
        col_i = sb("col_i", [P, 1])
        row8 = sb("row8", [NG, NG])

        x_sb = sb("x_sb", [P, TH, D])
        xn = sb("xn", [P, TH, D])
        xnT = sb("xnT", [P, DC, TOK])
        stats = sb("stats", [P, TH, 6])
        meanvar = sb("meanvar", [P, TH, 2])
        rstd = sb("rstd", [P, TH])
        var_eps = sb("var_eps", [P, TH])
        root_t = sb("root_t", [P, TH])

        mask_u8 = sb("mask_u8", [NG, GRP], U8)
        bias8 = sb("bias8", [NG, GRP])
        bias_g = sb("bias_g", [NG, GRP], BF16)
        flag = sb("flag", [NG, 1])
        flag_b = sb("flag_b", [NG, 1], BF16)
        col_b = sb("col_b", [NG, 1], BF16)
        pick = sb("pick", [NG, NG])
        pick_b = sb("pick_b", [NG, NG], BF16)
        plan = sb("plan", [1, 16], I32)
        any_valid = sb("any_valid", [P, 1])

        GU_W = DC * INTER
        SLOT_W = 2 * GU_W + 2 * D
        ring = sb("ring", [P, RING, 2, SLOT_W])
        RING_W = RING * 2 * SLOT_W
        XA_W = 13 * 1024
        arena = ring[:, :, :, :].rearrange("p r e n -> p (r e n)")[:, RING_W - XA_W:]
        RING_FREE = (RING_W - XA_W) // (2 * SLOT_W)
        off = [0]

        def carve(shape, dt=F32):
            n = int(np.prod(shape[1:])) * (4 if dt == F32 else 2) // 4
            assert off[0] + n <= arena.shape[1], (off, n)
            a = arena[:, off[0]:off[0] + n]
            off[0] += n
            if dt != F32:
                a = a.bitcast(dt)
            if len(shape) == 3:
                a = a.rearrange("p (a b) -> p a b", a=shape[1])
            if len(shape) == 4:
                a = a.rearrange("p (a b c) -> p a b c", a=shape[1], b=shape[2])
            if len(shape) == 5:
                a = a.rearrange("p (a b c d) -> p a b c d", a=shape[1], b=shape[2], c=shape[3])
            return a

        ctx_k = carve([P, KC, D])
        ctx_v = carve([P, 2, KC, D])
        ctxT = carve([P, DC, GRP])
        probs = carve([P, TH, GRP])
        probsT = carve([P, TH, KC, P])
        o_acc = carve([P, TH, D])
        m_run = sb("m_run", [P, TH])
        m_new = sb("m_new", [P, TH])
        m_grp = sb("m_grp", [P, TH])
        m_diff = sb("m_diff", [P, TH])
        nbias = sb("nbias", [P, TH])
        alpha = sb("alpha", [P, TH])
        r_sum = sb("r_sum", [P, TH])
        l_run = sb("l_run", [P, TH])
        o_scale = sb("o_scale", [P, TH])

        assert off[0] <= XA_W

        arena = sb("arena2", [P, 22016])[:, :]
        off[0] = 0
        wqkv_sb = carve([P, DC, 3 * D])
        wout_sb = carve([P, DC, D])
        qk_n = carve([P, TH, 2 * D])
        squares = carve([P, TH, 2 * D])
        rot = carve([P, 4, 256])
        v_sb = carve([P, TH, D])
        qkT = carve([P, HG, 2 * TOK])
        s_probs = carve([P, 2, 4, 3 * P])
        s_probsT = carve([P, 3, 4, P])
        y_sb = carve([P, TH, D])
        off[0] = 0
        xparts = carve([P, TH, 3, DC, P], BF16)
        chosen = carve([P, TH, EXP_N])
        chosen_b = carve([P, TH, EXP_N], BF16)
        rexp = carve([P, TH, EXP_N])
        rw = carve([P, TH, EXP_N])
        rank = carve([P, TH, EXP_N])
        pick_t = carve([P, TH, 2, BLK], BF16)
        apart = carve([P, TH, 2, BLK])
        mix_t = carve([P, TH, 2, BLK])
        mixT = carve([P, TOK])
        xs = carve([P, DC, P])
        silu = carve([P, INTER])
        hid = carve([P, INTER])
        hidT = carve([P, 2, P])
        y_slot = carve([P, D])

        cs_sb = sb("cs_sb", [P, TH, 2, HD // 2])
        gain_sb = sb("gain_sb", [P, HEADS])
        gate_sb = sb("gate_sb", [P, DC, EXP_N])
        head_ss = sb("head_ss", [P, TH, 2 * HEADS])
        head_r = sb("head_r", [P, TH, 2 * HEADS])
        head_t = sb("head_t", [P, TH, 2 * HEADS])
        s_max = sb("s_max", [P, 2, TH * 4])
        s_nmax = sb("s_nmax", [P, 2, TH * 4])
        s_sum = sb("s_sum", [P, 2, TH * 4])
        s_inv = sb("s_inv", [P, 2, TH * 4])
        logits = sb("logits", [P, TH, EXP_N])
        top8 = sb("top8", [P, TH, 8])
        cut = sb("cut", [P, TH, EXP_N])
        ntop = sb("ntop", [P, TH])
        rsum = sb("rsum", [P, TH])
        cnt_i = sb("cnt_i", [1, PAIRS], I32)
        rounds = sb("rounds", [1, PAIRS], I32)

        s_x = sem("x_loaded")
        s_mask = sem("mask_loaded")
        s_const = sem("constants_ready")
        s_gpc = sem("gpsimd_chain")
        s_dve = sem("dve_chain")
        s_dvl = sem("dve_loop_chain")
        s_flag = sem("flags_ready")
        s_pos = sem("positions_ready")
        s_pick = sem("pick_ready")
        s_list = sem("list_in_psum")
        s_plan = sem("plan_ready")
        s_xn = sem("normed_ready")
        s_xnt = sem("normedT_in_psum")
        s_xnT = sem("normedT_ready")
        s_ck = sem("ctx_k_loaded")
        s_cv = sem("ctx_v_loaded")
        s_t = sem("ctxT_in_psum")
        s_ta = sem("ctxT_copied_act")
        s_td = sem("ctxT_copied_dve")
        s_bias = sem("bias_ready")
        s_s = sem("scores_ready")
        s_nb = sem("neg_max_ready")
        s_p = sem("probs_ready")
        s_al = sem("alpha_ready")
        s_pt = sem("probsT_in_psum")
        s_ptc = sem("probsT_ready")
        s_o = sem("readout_in_psum")
        s_oc = sem("readout_added")
        s_x1 = sem("x1_ready")
        s_out = sem("out_stored")
        s_tables = sem("tables_ready")
        s_small = sem("angles_and_gain_loaded")
        s_wq = sem("w_qkv_loaded")
        s_wo = sem("w_out_loaded")
        s_gw = sem("gate_w_loaded")
        s_qkv = sem("qkv_in_psum")
        s_sq = sem("squares_ready")
        s_v = sem("values_ready")
        s_rot = sem("rotated_ready")
        s_qkp = sem("qkT_in_psum")
        s_qka = sem("qkT_copied_act")
        s_qkd = sem("qkT_copied_dve")
        s_sc = sem("self_scores_ready")
        s_nm = sem("self_neg_max_ready")
        s_e = sem("self_probs_ready")
        s_spt = sem("self_probsT_in_psum")
        s_spa = sem("self_probsT_copied_act")
        s_spd = sem("self_probsT_copied_dve")
        s_pv = sem("self_values_in_psum")
        s_yn = sem("heads_normed")
        s_ytp = sem("yT_in_psum")
        s_yta = sem("yT_copied_act")
        s_ytd = sem("yT_copied_dve")
        s_op = sem("projection_in_psum")
        s_x2 = sem("x2_ready")
        s_lg = sem("logits_in_psum")
        s_tv = sem("top_values_ready")
        s_ex = sem("router_exp_ready")
        s_ch = sem("chosen_ready")
        s_rw = sem("router_weights_ready")
        s_rank = sem("ranks_in_psum")
        s_xp1 = sem("first_parts_ready")
        s_xr1 = sem("first_rest_ready")
        s_xp2 = sem("second_parts_ready")
        s_xp = sem("third_parts_ready")
        s_cnt = sem("rounds_ready")
        s_rk = sem("rank_table_ready")
        s_ap = sem("rank_less_slot_ready")
        s_pk = sem("pick_written")
        s_gpr = sem("ranks_moved_on")
        s_mx = sem("mix_written")
        s_mtp = sem("mixT_in_psum")
        s_mt = sem("mixT_ready")
        s_xg = sem("gathered_in_psum")
        s_xgc = sem("gathered_ready")
        s_w = [sem(f"weights_loaded_{r}") for r in range(RING)]
        s_gu = sem("gate_up_in_psum")
        s_si = sem("silu_ready")
        s_h = sem("hidden_ready")
        s_htp = sem("hiddenT_in_psum")
        s_ht = sem("hiddenT_ready")
        s_y = sem("expert_out_in_psum")
        s_yc = sem("expert_out_copied")
        s_mm = sem("outputs_mixed")
        s_fin = sem("result_ready")

        block = es.enter_context(nc.Block())

        QK_BANKS = (6, 7, 0, 1)
        PT_BANKS = (6, 7, 0)

        class Chain:
            def __init__(self, eng, s, base=0):
                self.eng, self.s, self.base, self.n = eng, s, base, 0

            def step(self, ins, wait=True):
                self.n += 1
                ins.then_inc(self.s, 1)
                if wait:
                    self.wait()

            def wait(self):
                self.eng.wait_ge(self.s, self.base + self.n)

        ctx_rows = ctxm[0].rearrange("(g c p) d -> g p c d", g=NG, p=P)

        @block.sync
        def _(sp):
            sp.dma_start(mask_u8[:, :], mask[0].rearrange("(g n) -> g n", g=NG)).then_inc(s_mask, 16)
            sp.dma_start(x_sb[:, :, :], x[0].rearrange("(h p) d -> p h d", p=P)).then_inc(s_x, 16)
            sp.wait_ge(s_plan, 1)
            n = sp.value_load(plan[0:1, 15:16], min_val=1, max_val=NG)
            g = sp.value_load(plan[0:1, 0:1], min_val=0, max_val=NG - 1)
            sp.dma_start(ctx_k, ctx_rows[g]).then_inc(s_ck, 16)
            with sp.Fori(0, n) as i:
                gv = sp.value_load(plan[0:1, bass.ds(i, 1)], min_val=0, max_val=NG - 1)
                sp.wait_ge(s_oc, 2 * i + 1)
                sp.dma_start(ctx_v[:, bass.ds(i % 2, 1)], ctx_rows[gv]).then_inc(s_cv, 16)
                gk = sp.value_load(plan[0:1, bass.ds(i + 1, 1)], min_val=0, max_val=NG - 1)
                sp.wait_ge(s_t, DC * (i + 1))
                sp.dma_start(ctx_k, ctx_rows[gk]).then_inc(s_ck, 16)

            def load_pair(u, r):
                pair = bass.ds(2 * u, 2)
                for dst, src in ((ring[:, r, :, 0:GU_W], gate_proj[pair].rearrange("e (p c) n -> p e (c n)", c=DC)),
                                 (ring[:, r, :, GU_W:2 * GU_W], up_proj[pair].rearrange("e (p c) n -> p e (c n)", c=DC)),
                                 (ring[0:HALF_I, r, :, 2 * GU_W:], down_proj[pair].rearrange("e (p k) n -> p e (k n)", k=2))):
                    sp.dma_start(dst, src).then_inc(s_w[r], 16)

            for r in range(RING):
                if r == RING_FREE:
                    sp.wait_ge(s_x1, 2)
                load_pair(r, r)
            sp.wait_ge(s_cnt, 1)
            done = sp.alloc_register("sp_done")
            sp.reg_mov(done, 0)
            with sp.Fori(0, LAPS - 1) as lap:
                for r in range(RING):
                    last = sp.value_load(rounds[0:1, bass.ds(lap * RING + r, 1)], min_val=1, max_val=TOK // BLK)
                    sp.reg_add(done, done, last)
                    sp.wait_ge(s_y, sp.snap(done))
                    load_pair(lap * RING + RING + r, r)
            for h in range(TH):
                sp.wait_ge(s_fin, h + 1)
                sp.dma_start(out[0, h * P:(h + 1) * P, :], x_sb[:, h]).then_inc(s_out, 16)
            sp.wait_ge(s_out, 32)

        @block.gpsimd
        def _(pool):
            ch = Chain(pool, s_gpc)
            ch.step(pool.memset(ident[:, :], 0.0), wait=False)
            ch.step(pool.memset(ones_b[:, :], 1.0), wait=False)
            ch.step(pool.memset(ident_b[:, :], 0.0), wait=False)
            ch.step(pool.memset(causal_b[:, :, :], 0.0), wait=False)
            ch.step(pool.memset(later_b[:, :, :], 1.0), wait=True)
            pool.affine_select(out=ident[:, :], in_=ident[:, :], compare_op=ALU.not_equal, fill=1.0,
                               base=0, pattern=[[-1, P]], channel_multiplier=1).then_inc(s_const, 1)
            pool.affine_select(out=later_b[:, :, :], in_=later_b[:, :, :], compare_op=ALU.is_gt, fill=0.0,
                               base=0, pattern=[[-P, TH], [1, TOK]], channel_multiplier=-1).then_inc(s_const, 1)
            pool.iota(col_i[:, :], pattern=[[0, 1]], base=0, channel_multiplier=1,
                      allow_small_or_imprecise_dtypes=True).then_inc(s_const, 1)
            pool.iota(row8[:, :], pattern=[[1, NG]], base=0, channel_multiplier=0,
                      allow_small_or_imprecise_dtypes=True).then_inc(s_const, 1)
            pool.affine_select(out=ident_b[:, :], in_=ident_b[:, :], compare_op=ALU.not_equal, fill=1.0,
                               base=0, pattern=[[-1, P]], channel_multiplier=1).then_inc(s_tables, 1)
            pool.affine_select(out=causal_b[:, 1:3, :], in_=causal_b[:, 1:3, :], compare_op=ALU.is_ge, fill=-BIG,
                               base=0, pattern=[[0, 2], [-1, P]], channel_multiplier=1).then_inc(s_tables, 1)
            pool.memset(blk_c[:, :, :], float(BLK)).then_inc(s_tables, 1)
            pool.iota(slot_row[:, :], pattern=[[1, BLK]], base=0, channel_multiplier=0,
                      allow_small_or_imprecise_dtypes=True).then_inc(s_tables, 1)

            pool.wait_ge(s_tables, 4)
            pool.wait_ge(s_cnt, 1)
            pool.wait_ge(s_rk, 1)
            pool.wait_ge(s_rw, 1)
            step = pool.alloc_register("pool_step")
            pool.reg_mov(step, 0)
            slots = slot_row[:, :].unsqueeze(1).unsqueeze(1).to_broadcast([P, TH, 2, BLK])

            def over_slots(table, u):
                return table[:, :, bass.ds(2 * u, 2)].unsqueeze(3).to_broadcast([P, TH, 2, BLK])

            with pool.Fori(0, PAIRS) as u:
                count = pool.value_load(rounds[0:1, bass.ds(u, 1)], min_val=1, max_val=TOK // BLK)
                with pool.Fori(0, count):
                    v = pool.snap(step)
                    pool.wait_ge(s_pk, v + 1)
                    pool.wait_ge(s_gpr, v + 1)
                    pool.tensor_tensor(apart, over_slots(rank, u), slots, ALU.subtract).then_inc(s_ap, 1)
                    pool.wait_ge(s_pk, v + 2)
                    pool.wait_ge(s_mtp, v + 1)
                    pool.tensor_tensor(mix_t, pick_t, over_slots(rw, u), ALU.mult).then_inc(s_mx, 1)
                    left = rank[:, :, bass.ds(2 * u, 2)]
                    pool.tensor_tensor(left, left, blk_c[:, :, :], ALU.subtract).then_inc(s_gpr, 1)
                    pool.reg_add(step, step, 1)
            pool.wait_ge(s_pk, pool.snap(step) + 1)
            pool.tensor_tensor(apart, apart, apart, ALU.subtract).then_inc(s_ap, 1)

        def inverse_root(dve, ch, y, v, t):
            yi, vi = y.bitcast(I32), v.bitcast(I32)
            ch.step(dve.tensor_scalar(yi, vi, 1, None, ALU.logical_shift_right))
            ch.step(dve.tensor_scalar(yi, yi, -1.0, float(0x5F3759DF), ALU.mult, ALU.add))
            for _ in range(3):
                ch.step(dve.tensor_tensor(t, y, y, ALU.mult))
                ch.step(dve.scalar_tensor_tensor(t, t, -0.5, v, ALU.mult, ALU.mult))
                ch.step(dve.scalar_tensor_tensor(y, t, 1.5, y, ALU.add, ALU.mult))

        def layer_norm(dve, ch):
            for h in range(TH):
                ch.step(dve.bn_stats(stats[:, h, :], x_sb[:, h, :]), wait=False)
            ch.wait()
            for h in range(TH):
                ch.step(dve.bn_aggr(meanvar[:, h, :], stats[:, h, :]), wait=False)
            ch.wait()
            ch.step(dve.tensor_scalar(var_eps[:, :], meanvar[:, :, 1], EPS_LN, None, ALU.add))
            inverse_root(dve, ch, rstd[:, :], var_eps[:, :], root_t[:, :])
            for h in range(TH):
                dve.tensor_scalar(xn[:, h, :], x_sb[:, h, :], meanvar[:, h, 0:1], rstd[:, h:h + 1],
                                  ALU.subtract, ALU.mult).then_inc(s_xn, 1)

        def transpose_xn(pe, banks):
            for c in range(DC):
                for h in range(TH):
                    last = pe.transpose(banks[c // 2][:, (c % 2) * TOK + h * P:(c % 2) * TOK + (h + 1) * P],
                                        xn[:, h, c::DC], ident[:, :])
                if c % 2:
                    last.then_inc(s_xnt, 1)

        def copy_xnT(dve, done, b):
            for j in range(2):
                dve.wait_ge(s_xnt, done + j + 1)
                dve.tensor_copy(xnT[:, 2 * j:2 * j + 2, :],
                                bank[b + j].rearrange("p (c t) -> p c t", c=2)).then_inc(s_xnT, 1)

        @block.vector
        def _(dve):
            ch = Chain(dve, s_dve)
            for h in range(TH):
                dve.memset(o_acc[:, h], 0.0).then_inc(s_oc, 1)
            dve.memset(alpha[:, :], 0.0).then_inc(s_oc, 1)
            ch.step(dve.memset(l_run[:, :], 0.0), wait=False)
            ch.step(dve.memset(m_run[:, :], LOWEST), wait=False)
            dve.wait_ge(s_const, 4)
            ch.step(dve.tensor_copy(col_b[:, :], col_i[0:NG, :]), wait=False)
            dve.wait_ge(s_mask, 16)
            ch.step(dve.tensor_reduce(flag[:, :], mask_u8[:, :], AX.X, ALU.max))
            dve.tensor_copy(flag_b[:, :], flag[:, :]).then_inc(s_flag, 1)
            ch.step(dve.tensor_scalar(bias8[:, :], mask_u8[:, :], 1.0, BIG, ALU.subtract, ALU.mult))
            dve.wait_ge(s_pos, 1)
            ch.step(dve.tensor_scalar(pick[:, :], row8[:, :], bank[7][0:NG, 0:1], flag[:, :],
                                      ALU.is_equal, ALU.mult))
            dve.tensor_copy(pick_b[:, :], pick[:, :]).then_inc(s_pick, 1)
            ch.step(dve.tensor_scalar(any_valid[:, :], bank[7][:, 1:2], 1.0, None, ALU.min), wait=False)
            ch.step(dve.memset(plan[:, :], 0))
            dve.wait_ge(s_list, 1)
            ch.step(dve.tensor_copy(plan[0:1, 0:NG], bank[6][0:1, 0:NG]), wait=False)
            dve.tensor_scalar(plan[0:1, 15:16], bank[7][0:1, 1:2], 1.0, None, ALU.max).then_inc(s_plan, 1)
            dve.wait_ge(s_x, 16)
            layer_norm(dve, ch)
            copy_xnT(dve, 0, 4)

            def copy_ctxT(k):
                for c in (2, 3):
                    dve.wait_ge(s_t, DC * k + c + 1)
                    dve.tensor_copy(ctxT[:, c, :], bank[c][:, :]).then_inc(s_td, 1)

            dve.wait_ge(s_plan, 1)
            n = dve.value_load(plan[0:1, 15:16], min_val=1, max_val=NG)
            copy_ctxT(0)
            STEPS = 10
            with dve.Fori(0, n) as i:
                lc = Chain(dve, s_dvl, base=i * STEPS)
                dve.tensor_scalar(bias_g[:, :], bias8[:, :], pick[:, bass.ds(i, 1)], None, ALU.mult).then_inc(s_bias, 1)
                for h in range(TH):
                    hs = slice(h, h + 1)
                    dve.wait_ge(s_s, 2 * i + h + 1)
                    lc.step(dve.tensor_reduce(m_grp[:, hs], bank[4 + h][:, :], AX.X, ALU.max))
                    lc.step(dve.tensor_tensor(m_new[:, hs], m_run[:, hs], m_grp[:, hs], ALU.max))
                    lc.step(dve.tensor_tensor(m_diff[:, hs], m_run[:, hs], m_new[:, hs], ALU.subtract), wait=False)
                    dve.tensor_scalar(nbias[:, hs], m_new[:, hs], -XSCALE, None, ALU.mult).then_inc(s_nb, 1)
                    lc.wait()
                    lc.step(dve.tensor_copy(m_run[:, hs], m_new[:, hs]), wait=False)
                copy_ctxT(i + 1)
                for h in range(TH):
                    dve.wait_ge(s_pt, 2 * i + h + 1)
                    dve.tensor_copy(probsT[:, h], bank[6 + h][:, :].rearrange("p (k t) -> p k t", k=KC)).then_inc(s_ptc, 1)
                for h in range(TH):
                    hs = slice(h, h + 1)
                    dve.wait_ge(s_al, 2 * i + h + 1)
                    dve.wait_ge(s_p, 2 * i + h + 1)
                    lc.step(dve.scalar_tensor_tensor(l_run[:, hs], l_run[:, hs], alpha[:, hs], r_sum[:, hs],
                                                     ALU.mult, ALU.add), wait=False)
                    dve.wait_ge(s_o, 2 * i + h + 1)
                    dve.scalar_tensor_tensor(o_acc[:, h], o_acc[:, h], alpha[:, hs], bank[4 + h][:, :],
                                             ALU.mult, ALU.add).then_inc(s_oc, 1)
                lc.wait()
                assert lc.n == STEPS, lc.n
            dve.wait_ge(s_oc, 2 * n + 3)
            dve.wait_ge(s_ta, 2 * n + 2)
            ch.step(dve.reciprocal(o_scale[:, :], l_run[:, :]))
            ch.step(dve.tensor_scalar(o_scale[:, :], o_scale[:, :], any_valid[:, :], None, ALU.mult))
            for h in range(TH):
                dve.scalar_tensor_tensor(x_sb[:, h], o_acc[:, h], o_scale[:, h:h + 1], x_sb[:, h],
                                         ALU.mult, ALU.add).then_inc(s_x1, 1)

            dve.wait_ge(s_x1, 2)
            layer_norm(dve, ch)
            copy_xnT(dve, 2, 6)
            dve.wait_ge(s_small, 32)
            for h in range(TH):
                dve.wait_ge(s_sq, 2 * h + 2)
                ch.step(dve.tensor_reduce(head_ss[:, h], squares[:, h].rearrange("p (a d) -> p a d", d=HD), AX.X, ALU.add))
                ch.step(dve.tensor_scalar(head_ss[:, h], head_ss[:, h], EPS_UNIT, None, ALU.add))
                inverse_root(dve, ch, head_r[:, h], head_ss[:, h], head_t[:, h])
                ch.step(dve.tensor_tensor(head_r[:, h, 0:HEADS], head_r[:, h, 0:HEADS], gain_sb[:, :], ALU.mult))
                for j in range(2):
                    ch.step(dve.tensor_tensor(
                        qk_n[:, h, j * D:(j + 1) * D].rearrange("p (a d) -> p a d", d=HD),
                        bank[3 * h + j].rearrange("p (a d) -> p a d", d=HD),
                        head_r[:, h, j * HEADS:(j + 1) * HEADS].unsqueeze(2).to_broadcast([P, HEADS, HD]),
                        ALU.mult), wait=False)
                ch.wait()
                even = qk_n[:, h].rearrange("p (a d) -> p a d", d=2 * HD)
                t1, t2 = even[:, :, 0:HD // 2], even[:, :, HD // 2:HD]
                cos = cs_sb[:, h, 0, :].unsqueeze(1).to_broadcast([P, HEADS, HD // 2])
                sin = cs_sb[:, h, 1, :].unsqueeze(1).to_broadcast([P, HEADS, HD // 2])
                parts = [rot[:, n].rearrange("p (a d) -> p a d", d=HD // 2) for n in range(4)]
                for dst, t, f in zip(parts, (t1, t2, t1, t2), (cos, sin, sin, cos)):
                    ch.step(dve.tensor_tensor(dst, t, f, ALU.mult), wait=False)
                ch.wait()
                ch.step(dve.tensor_tensor(t1, parts[0], parts[1], ALU.subtract), wait=False)
                dve.tensor_tensor(t2, parts[2], parts[3], ALU.add).then_inc(s_rot, 1)
                ch.wait()
            for g in (1, 3):
                dve.wait_ge(s_qkp, g + 1)
                dve.tensor_copy(qkT[:, g, :], bank[QK_BANKS[g]]).then_inc(s_qkd, 1)

            def row_max(g):
                b = g % 2
                dve.wait_ge(s_sc, 4 * g + 4)
                ch.step(dve.tensor_reduce(s_max[:, b, 4:8], psum[:, 2:6, 0:2 * P], AX.X, ALU.max), wait=False)
                ch.step(dve.tensor_reduce(s_max[:, b, 0:4], psum[:, 2:6, 2 * P:3 * P], AX.X, ALU.max))
                dve.tensor_scalar(s_nmax[:, b, :], s_max[:, b, :], -1.0, None, ALU.mult).then_inc(s_nm, 1)

            row_max(0)
            for g in range(HG):
                if g:
                    dve.wait_ge(s_pv, g)
                for j in (1, 2):
                    dve.wait_ge(s_spt, 3 * g + j + 1)
                    dve.tensor_copy(s_probsT[:, j], bank[PT_BANKS[j]].rearrange("p (r t) -> p r t", r=4)).then_inc(s_spd, 1)
                if g + 1 < HG:
                    row_max(g + 1)
                dve.wait_ge(s_e, 8 * g + 8)
                ch.step(dve.reciprocal(s_inv[:, g % 2], s_sum[:, g % 2]))
                dve.wait_ge(s_pv, g + 1)
                for h in range(TH):
                    ins = dve.tensor_tensor(
                        y_sb[:, h, g * P:(g + 1) * P].rearrange("p (r d) -> p r d", r=4),
                        bank[1][:, h * P:(h + 1) * P].rearrange("p (r d) -> p r d", r=4),
                        s_inv[:, g % 2, 4 * h:4 * h + 4].unsqueeze(2).to_broadcast([P, 4, HD]), ALU.mult)
                    ins.then_inc(s_yn, 1)
            dve.wait_ge(s_ytp, 2)
            dve.tensor_copy(xnT[:, 2:4, :], bank[3].rearrange("p (c t) -> p c t", c=2)).then_inc(s_ytd, 1)
            for h in range(TH):
                dve.wait_ge(s_op, h + 1)
                dve.tensor_tensor(x_sb[:, h], x_sb[:, h], bank[4 + h], ALU.add).then_inc(s_x2, 1)

            dve.wait_ge(s_x2, 2)
            layer_norm(dve, ch)
            copy_xnT(dve, 4, 6)
            rest = xn
            dve.wait_ge(s_xp1, 2)
            for h in range(TH):
                dve.tensor_tensor(rest[:, h].rearrange("p (q c) -> p c q", c=DC), xn[:, h].rearrange("p (q c) -> p c q", c=DC),
                                  xparts[:, h, 0], ALU.subtract).then_inc(s_xr1, 1)
            dve.wait_ge(s_lg, 1)
            ch.step(dve.tensor_copy(logits[:, :, :], bank[0][:, 0:TH * EXP_N].rearrange("p (h e) -> p h e", h=TH)))
            for h in range(TH):
                ch.step(dve.max(top8[:, h], logits[:, h]), wait=False)
            ch.wait()
            dve.tensor_scalar(ntop[:, :], top8[:, :, 0], -1.0, None, ALU.mult).then_inc(s_tv, 1)
            for h in range(TH):
                ch.step(dve.match_replace(cut[:, h], top8[:, h], logits[:, h], LOWEST), wait=False)
            ch.wait()
            ch.step(dve.tensor_tensor(chosen, cut[:, :, :], logits[:, :, :], ALU.not_equal))
            dve.tensor_copy(chosen_b, chosen).then_inc(s_ch, 1)
            dve.wait_ge(s_rank, 1)
            ch.step(dve.scalar_tensor_tensor(rank, bank[1][:, 0:TH * EXP_N].rearrange("p (h e) -> p h e", h=TH), 1.0,
                                             chosen, ALU.add, ALU.mult))
            dve.tensor_scalar(rank, rank, 1.0, None, ALU.subtract).then_inc(s_rk, 1)
            ch.step(dve.tensor_reduce(cnt_i[:, :], bank[2][0:1, 0:EXP_N].rearrange("p (u e) -> p u e", e=2), AX.X, ALU.max))
            ch.step(dve.tensor_scalar(cnt_i[:, :], cnt_i[:, :], float(BLK - 1), None, ALU.add))
            ch.step(dve.tensor_scalar(cnt_i[:, :], cnt_i[:, :], 6, None, ALU.arith_shift_right))
            dve.tensor_scalar(rounds[:, :], cnt_i[:, :], 1.0, None, ALU.max).then_inc(s_cnt, 1)
            dve.memset(mixT, 0.0).then_inc(s_mt, 1)
            dve.memset(y_slot, 0.0).then_inc(s_yc, 1)
            dve.memset(pick_t, 0.0).then_inc(s_pk, 1)
            dve.memset(mix_t, 0.0).then_inc(s_mtp, 1)
            dve.memset(hidT, 0.0).then_inc(s_gpr, 1)
            dve.wait_ge(s_xp2, 2)
            for h in range(TH):
                dve.tensor_tensor(xparts[:, h, 2], rest[:, h].rearrange("p (q c) -> p c q", c=DC),
                                  xparts[:, h, 1], ALU.subtract).then_inc(s_xp, 1)
            dve.wait_ge(s_ex, 2)
            ch.step(dve.tensor_tensor(rexp, rexp, chosen, ALU.mult))
            ch.step(dve.tensor_reduce(rsum[:, :], rexp, AX.X, ALU.add))
            ch.step(dve.reciprocal(rsum[:, :], rsum[:, :]))
            dve.tensor_tensor(rw, rexp, rsum[:, :].unsqueeze(2).to_broadcast([P, TH, EXP_N]), ALU.mult).then_inc(s_rw, 1)

            def write_pick():
                dve.tensor_scalar(pick_t, apart, 0.0, None, ALU.is_equal).then_inc(s_pk, 1)

            dve.wait_ge(s_pk, 1)
            dve.wait_ge(s_ap, 1)
            write_pick()
            step = dve.alloc_register("dve_step")
            dve.reg_mov(step, 0)
            with dve.Fori(0, PAIRS) as u:
                count = dve.value_load(rounds[0:1, bass.ds(u, 1)], min_val=1, max_val=TOK // BLK)
                with dve.Fori(0, count):
                    v = dve.snap(step)
                    dve.wait_ge(s_ap, v + 2)
                    dve.wait_ge(s_xg, v + 1)
                    dve.wait_ge(s_mx, v + 1)
                    write_pick()
                    dve.wait_ge(s_si, v + 1)
                    dve.tensor_tensor(hid, silu, bank[0][:, INTER:2 * INTER], ALU.mult).then_inc(s_h, 1)
                    dve.wait_ge(s_htp, v + 1)
                    dve.tensor_copy(hidT[0:HALF_I], bank[1][0:HALF_I, 0:2 * P].rearrange("p (k s) -> p k s", k=2)).then_inc(s_ht, 1)
                    dve.wait_ge(s_mtp, v + 2)
                    dve.wait_ge(s_y, v + 1)
                    dve.tensor_copy(mixT, bank[2][:, 0:TOK]).then_inc(s_mt, 1)
                    dve.reg_add(step, step, 1)

            for h in range(TH):
                dve.wait_ge(s_mm, h + 1)
                dve.tensor_tensor(x_sb[:, h], x_sb[:, h], bank[4 + h], ALU.add).then_inc(s_fin, 1)

        @block.scalar
        def _(act):
            act.dma_start(cs_sb[:, :, :, :], rope_cs.rearrange("(h p) a d -> p h a d", p=P)).then_inc(s_small, 16)
            act.dma_start(gain_sb[:, :], q_gain.partition_broadcast(P)).then_inc(s_small, 16)
            act.wait_ge(s_plan, 1)
            n = act.value_load(plan[0:1, 15:16], min_val=1, max_val=NG)

            def copy_ctxT(k):
                for c in (0, 1):
                    act.wait_ge(s_t, DC * k + c + 1)
                    act.activation(ctxT[:, c, :], bank[c][:, :], ACT.Copy).then_inc(s_ta, 1)

            copy_ctxT(0)
            act.dma_start(wqkv_sb, w_qkv.rearrange("(p c) n -> p c n", c=DC)).then_inc(s_wq, 16)
            act.dma_start(wout_sb, w_out.rearrange("(p c) n -> p c n", c=DC)).then_inc(s_wo, 16)
            act.dma_start(gate_sb[:, :, :], gate_w.rearrange("(p c) n -> p c n", c=DC)).then_inc(s_gw, 16)
            with act.Fori(0, n) as i:
                for h in range(TH):
                    act.wait_ge(s_nb, 2 * i + h + 1)
                    act.activation(probs[:, h], bank[4 + h][:, :], ACT.Exp, bias=nbias[:, h:h + 1], scale=XSCALE,
                                   accum_out=r_sum[:, h:h + 1]).then_inc(s_p, 1)
                    act.activation(alpha[:, h:h + 1], m_diff[:, h:h + 1], ACT.Exp, scale=XSCALE).then_inc(s_al, 1)
                copy_ctxT(i + 1)

            for h in range(TH):
                for j in range(2):
                    act.wait_ge(s_qkv, 3 * h + j + 1)
                    act.activation(squares[:, h, j * D:(j + 1) * D], bank[3 * h + j], ACT.Square).then_inc(s_sq, 1)
                act.wait_ge(s_qkv, 3 * h + 3)
                act.activation(v_sb[:, h], bank[3 * h + 2], ACT.Copy).then_inc(s_v, 1)
            for g in (0, 2):
                act.wait_ge(s_qkp, g + 1)
                act.activation(qkT[:, g, :], bank[QK_BANKS[g]], ACT.Copy).then_inc(s_qka, 1)

            def self_exp(g):
                b = g % 2
                act.wait_ge(s_nm, g + 1)
                if g >= 2:
                    act.wait_ge(s_spt, 3 * (g - 1))
                for r in range(4):
                    act.activation(s_probs[:, b, r, 0:2 * P], bank[2 + r][:, 0:2 * P], ACT.Exp,
                                   bias=s_nmax[:, b, 4 + r:5 + r], accum_out=s_sum[:, b, 4 + r:5 + r]).then_inc(s_e, 1)
                    act.activation(s_probs[:, b, r, 2 * P:3 * P], bank[2 + r][:, 2 * P:3 * P], ACT.Exp,
                                   bias=s_nmax[:, b, r:r + 1], accum_out=s_sum[:, b, r:r + 1]).then_inc(s_e, 1)

            self_exp(0)
            for g in range(HG):
                if g:
                    act.wait_ge(s_pv, g)
                act.wait_ge(s_spt, 3 * g + 1)
                act.activation(s_probsT[:, 0], bank[PT_BANKS[0]].rearrange("p (r t) -> p r t", r=4), ACT.Copy).then_inc(s_spa, 1)
                if g + 1 < HG:
                    self_exp(g + 1)
            act.wait_ge(s_ytp, 1)
            act.activation(xnT[:, 0:2, :], bank[2].rearrange("p (c t) -> p c t", c=2), ACT.Copy).then_inc(s_yta, 1)

            for h in range(TH):
                act.wait_ge(s_xn, 4 + h + 1)
                act.activation(xparts[:, h, 0], xn[:, h].rearrange("p (q c) -> p c q", c=DC), ACT.Copy).then_inc(s_xp1, 1)
            for h in range(TH):
                act.wait_ge(s_xr1, h + 1)
                act.activation(xparts[:, h, 1], xn[:, h].rearrange("p (q c) -> p c q", c=DC), ACT.Copy).then_inc(s_xp2, 1)
            act.wait_ge(s_tv, 1)
            for h in range(TH):
                act.activation(rexp[:, h], logits[:, h], ACT.Exp, bias=ntop[:, h:h + 1]).then_inc(s_ex, 1)

            def copy_gathered():
                act.activation(xs, bank[3].rearrange("p (c s) -> p c s", c=DC), ACT.Copy).then_inc(s_xgc, 1)

            act.wait_ge(s_cnt, 1)
            act.wait_ge(s_xg, 1)
            copy_gathered()
            step = act.alloc_register("act_step")
            act.reg_mov(step, 0)
            with act.Fori(0, PAIRS) as u:
                count = act.value_load(rounds[0:1, bass.ds(u, 1)], min_val=1, max_val=TOK // BLK)
                with act.Fori(0, count):
                    v = act.snap(step)
                    act.wait_ge(s_gu, v + 1)
                    act.activation(silu, bank[0][:, 0:INTER], ACT.Silu).then_inc(s_si, 1)
                    act.wait_ge(s_xg, v + 2)
                    copy_gathered()
                    act.wait_ge(s_y, v + 1)
                    act.activation(y_slot, bank[6], ACT.Copy).then_inc(s_yc, 1)
                    act.reg_add(step, step, 1)

        @block.tensor
        def _(pe):
            pe.wait_ge(s_const, 4)
            pe.wait_ge(s_flag, 1)
            pe.matmul(bank[7][0:NG, 0:1], later_b[0:NG, 0, 0:NG], flag_b[:, :], start=True, stop=True)
            pe.matmul(bank[7][:, 1:2], ones_b[0:NG, :], flag_b[:, :], start=True, stop=True).then_inc(s_pos, 1)
            pe.wait_ge(s_pick, 1)
            pe.matmul(bank[6][0:1, 0:NG], col_b[:, :], pick_b[:, :], start=True, stop=True).then_inc(s_list, 1)
            pe.wait_ge(s_xn, 2)
            transpose_xn(pe, bank[4:6])
            pe.wait_ge(s_plan, 1)
            n = pe.value_load(plan[0:1, 15:16], min_val=1, max_val=NG)

            def transpose_ctx():
                for c in range(DC):
                    for k in range(KC):
                        last = pe.transpose(bank[c][:, k * P:(k + 1) * P], ctx_k[:, k, c::DC], ident[:, :])
                    last.then_inc(s_t, 1)

            pe.wait_ge(s_ck, 16)
            transpose_ctx()
            pe.wait_ge(s_xnT, 2)
            with pe.Fori(0, n) as i:
                pe.wait_ge(s_bias, i + 1)
                pe.wait_ge(s_ta, 2 * i + 2)
                pe.wait_ge(s_td, 2 * i + 2)
                for h in range(TH):
                    pe.wait_ge(s_oc, 2 * i + h + 2)
                    pe.matmul(bank[4 + h][:, :], ones_b[0:NG, :], bias_g[:, :], start=True, stop=False)
                    for c in range(DC):
                        last = pe.matmul(bank[4 + h][:, :], xnT[:, c, h * P:(h + 1) * P], ctxT[:, c, :],
                                         start=False, stop=(c == DC - 1))
                    last.then_inc(s_s, 1)
                pe.wait_ge(s_ck, 16 * (i + 2))
                transpose_ctx()
                for h in range(TH):
                    pe.wait_ge(s_p, 2 * i + h + 1)
                    for k in range(KC):
                        last = pe.transpose(bank[6 + h][:, k * P:(k + 1) * P], probs[:, h, k * P:(k + 1) * P], ident[:, :])
                    last.then_inc(s_pt, 1)
                pe.wait_ge(s_cv, 16 * (i + 1))
                for h in range(TH):
                    pe.wait_ge(s_ptc, 2 * i + h + 1)
                    for k in range(KC):
                        last = pe.matmul(bank[4 + h][:, :], probsT[:, h, k, :], ctx_v[:, bass.ds(i % 2, 1), k, :],
                                         start=(k == 0), stop=(k == KC - 1))
                    last.then_inc(s_o, 1)

            pe.wait_ge(s_tables, 2)
            pe.wait_ge(s_ta, 2 * n + 2)
            pe.wait_ge(s_xn, 4)
            transpose_xn(pe, bank[6:8])
            pe.wait_ge(s_xnT, 4)
            pe.wait_ge(s_wq, 16)
            for h in range(TH):
                for j in range(3):
                    for c in range(DC):
                        last = pe.matmul(bank[3 * h + j], xnT[:, c, h * P:(h + 1) * P], wqkv_sb[:, c, j * D:(j + 1) * D],
                                         start=(c == 0), stop=(c == DC - 1))
                    last.then_inc(s_qkv, 1)
            for h in range(TH):
                pe.wait_ge(s_rot, h + 1)
                for g in range(HG):
                    for j in range(2):
                        last = pe.transpose(bank[QK_BANKS[g]][:, j * TOK + h * P:j * TOK + (h + 1) * P],
                                            qk_n[:, h, j * D + g * P:j * D + (g + 1) * P], ident[:, :])
                    if h:
                        last.then_inc(s_qkp, 1)
            pe.wait_ge(s_v, 2)

            def self_scores(g):
                if g % 2 == 0:
                    pe.wait_ge(s_qka, g // 2 + 1)
                else:
                    pe.wait_ge(s_qkd, g // 2 + 1)
                for r in range(4):
                    if g:
                        pe.wait_ge(s_e, 8 * (g - 1) + 2 * r + 2)
                    rows = slice(HD * r, HD * (r + 1))
                    pe.matmul(bank[2 + r][:, 0:3 * P], ident_b[:, :], causal_b[:, :, :], start=True, stop=False)
                    pe.matmul(bank[2 + r][:, 0:2 * P], qkT[rows, g, P:2 * P], qkT[rows, g, TOK:TOK + 2 * P],
                              start=False, stop=False)
                    pe.matmul(bank[2 + r][:, 2 * P:3 * P], qkT[rows, g, 0:P], qkT[rows, g, TOK:TOK + P],
                              start=False, stop=True).then_inc(s_sc, 1)

            self_scores(0)
            pe.wait_ge(s_qka, 2)
            pe.wait_ge(s_qkd, 2)
            for g in range(HG):
                if g:
                    pe.wait_ge(s_spa, g)
                    pe.wait_ge(s_spd, 2 * g)
                for r in range(4):
                    pe.wait_ge(s_e, 8 * g + 2 * r + 2)
                    for j in range(3):
                        last = pe.transpose(bank[PT_BANKS[j]][:, r * P:(r + 1) * P],
                                            s_probs[:, g % 2, r, j * P:(j + 1) * P], ident[:, :])
                        if r == 3:
                            last.then_inc(s_spt, 1)
                if g + 1 < HG:
                    self_scores(g + 1)
                pe.wait_ge(s_spa, g + 1)
                pe.wait_ge(s_spd, 2 * g + 2)
                if g:
                    pe.wait_ge(s_yn, 2 * g)
                for r in range(4):
                    head = slice((4 * g + r) * HD, (4 * g + r + 1) * HD)
                    pe.matmul(bank[1][:, r * HD:(r + 1) * HD], s_probsT[:, 2, r, :], v_sb[:, 0, head],
                              start=True, stop=True)
                    for j in range(2):
                        last = pe.matmul(bank[1][:, P + r * HD:P + (r + 1) * HD], s_probsT[:, j, r, :], v_sb[:, j, head],
                                         start=(j == 0), stop=(j == 1))
                last.then_inc(s_pv, 1)
            pe.wait_ge(s_yn, 2 * HG)
            for c in range(DC):
                for h in range(TH):
                    last = pe.transpose(bank[2 + c // 2][:, (c % 2) * TOK + h * P:(c % 2) * TOK + (h + 1) * P],
                                        y_sb[:, h, c::DC], ident[:, :])
                if c % 2:
                    last.then_inc(s_ytp, 1)
            pe.wait_ge(s_yta, 1)
            pe.wait_ge(s_ytd, 1)
            pe.wait_ge(s_wo, 16)
            for h in range(TH):
                for c in range(DC):
                    last = pe.matmul(bank[4 + h], xnT[:, c, h * P:(h + 1) * P], wout_sb[:, c, :],
                                     start=(c == 0), stop=(c == DC - 1))
                last.then_inc(s_op, 1)

            pe.wait_ge(s_xn, 6)
            transpose_xn(pe, bank[6:8])
            pe.wait_ge(s_xnT, 6)
            pe.wait_ge(s_gw, 16)
            for h in range(TH):
                for c in range(DC):
                    last = pe.matmul(bank[0][:, h * EXP_N:(h + 1) * EXP_N], xnT[:, c, h * P:(h + 1) * P], gate_sb[:, c, :],
                                     start=(c == 0), stop=(c == DC - 1))
            last.then_inc(s_lg, 1)
            pe.wait_ge(s_ch, 1)
            for q in range(TH):
                for h in range(q + 1):
                    pe.matmul(bank[1][:, q * EXP_N:(q + 1) * EXP_N], later_b[:, h, q * P:(q + 1) * P], chosen_b[:, h],
                              start=(h == 0), stop=(h == q))
            for h in range(TH):
                last = pe.matmul(bank[2][0:1, 0:EXP_N], ones_b[:, 0:1], chosen_b[:, h], start=(h == 0), stop=(h == TH - 1))
            last.then_inc(s_rank, 1)

            def gather():
                for c in range(DC):
                    for k, (part, h) in enumerate((part, h) for part in range(3) for h in range(TH)):
                        last = pe.matmul(bank[3][:, c * P:(c + 1) * P], xparts[:, h, part, c, :], pick_t[:, h],
                                         start=(k == 0), stop=(k == 3 * TH - 1))
                last.then_inc(s_xg, 1)

            def mix(start=False, stop=False):
                for h in range(TH):
                    last = pe.matmul(bank[4 + h], mixT[:, h * P:(h + 1) * P], y_slot, start=start, stop=stop)
                    if stop:
                        last.then_inc(s_mm, 1)

            pe.wait_ge(s_cnt, 1)
            pe.wait_ge(s_mt, 1)
            pe.wait_ge(s_yc, 1)
            mix(start=True)
            pe.wait_ge(s_xp, 2)
            pe.wait_ge(s_pk, 2)
            gather()
            step = pe.alloc_register("pe_step")
            pe.reg_mov(step, 0)
            with pe.Fori(0, LAPS) as lap:
                for r in range(RING):
                    pe.wait_ge(s_w[r], 48 * (lap + 1))
                    count = pe.value_load(rounds[0:1, bass.ds(lap * RING + r, 1)], min_val=1, max_val=TOK // BLK)
                    with pe.Fori(0, count):
                        v = pe.snap(step)
                        pe.wait_ge(s_xgc, v + 1)
                        for c in range(DC):
                            for e in range(2):
                                half = slice(e * BLK, (e + 1) * BLK)
                                w = ring[:, r, e, 0:2 * GU_W].rearrange("p (g c n) -> p g c n", g=2, c=DC)
                                last = pe.matmul(bank[0][half, 0:2 * INTER], xs[:, c, half], w[:, :, c, :],
                                                 start=(c == 0), stop=(c == DC - 1))
                        last.then_inc(s_gu, 1)
                        pe.wait_ge(s_pk, v + 3)
                        gather()
                        pe.wait_ge(s_mx, v + 1)
                        pe.wait_ge(s_mt, v + 1)
                        for h in range(TH):
                            last = pe.transpose(bank[2][:, h * P:(h + 1) * P], mix_t[:, h].rearrange("p e s -> p (e s)"), ident[:, :])
                        last.then_inc(s_mtp, 1)
                        pe.wait_ge(s_h, v + 1)
                        for k in range(2):
                            last = pe.transpose(bank[1][0:HALF_I, k * P:(k + 1) * P], hid[:, k::2], ident[:, :])
                        last.then_inc(s_htp, 1)
                        pe.wait_ge(s_yc, v + 1)
                        mix()
                        pe.wait_ge(s_ht, v + 1)
                        for k in range(2):
                            for e in range(2):
                                half = slice(e * BLK, (e + 1) * BLK)
                                last = pe.matmul(bank[6][half, :], hidT[0:HALF_I, k, half],
                                                 ring[0:HALF_I, r, e, 2 * GU_W + k * D:2 * GU_W + (k + 1) * D],
                                                 start=(k == 0), stop=(k == 1))
                        last.then_inc(s_y, 1)
                        pe.reg_add(step, step, 1)
            pe.wait_ge(s_yc, pe.snap(step) + 1)
            pe.wait_ge(s_mt, pe.snap(step) + 1)
            mix(stop=True)


_INS = ['x', 'ctx_2048', 'mask_BxS2_bk0', 'L0_attn_w_qkv', 'L0_attn_w_out', 'L0_attn_q_gain', 'L0_ffn_gate_w',
        'L0_ffn_gate_proj_w', 'L0_ffn_up_proj_w', 'L0_ffn_down_proj_w']


def kernel(**inputs):
    import numpy as _np
    import concourse.bacc as _bacc
    from concourse import mybir as _mybir
    from concourse.bass_utils import run_bass_kernel_spmd as _run

    nc = _bacc.Bacc("TRN2", target_bir_lowering=False, num_devices=1)
    arrays, args = {}, []
    for name in _INS:
        a = _np.ascontiguousarray(inputs[name])
        arrays[f"in_{name}_dram"] = a
        args.append(nc.dram_tensor(f"in_{name}_dram", a.shape, _mybir.dt.from_np(a.dtype), kind="ExternalInput").ap())
    inv_freq = _np.float32(10000.0) ** (-_np.arange(HD // 2, dtype=_np.float32) / _np.float32(HD // 2))
    theta = _np.arange(TOK, dtype=_np.float32)[:, None] * inv_freq[None, :]
    arrays["rope_dram"] = _np.stack([_np.cos(theta), _np.sin(theta)], axis=1).astype(_np.float32)
    args.append(nc.dram_tensor("rope_dram", (TOK, 2, HD // 2), _mybir.dt.float32, kind="ExternalInput").ap())
    args.append(nc.dram_tensor("out_0_dram", (1, TOK, D), _mybir.dt.float32, kind="ExternalOutput").ap())
    perceiver(nc, *args)
    r = _run(nc, [arrays], core_ids=[0])
    return r.results[0]["out_0_dram"]
```

```python
import numpy as np
import concourse.bass as bass
from concourse import mybir
from contextlib import ExitStack

F32 = mybir.dt.float32
BF16 = mybir.dt.bfloat16
I32 = mybir.dt.int32
U8 = mybir.dt.uint8
ALU = mybir.AluOpType
ACT = mybir.ActivationFunctionType
AX = mybir.AxisListType

P = 128
TOK, D = 256, 512
TH = TOK // P
DC = D // P
MEM = 4096
GRP = 512
NG = MEM // GRP
KC = GRP // P
HEADS, HD = 16, 32
HG = 4
EXP_N, TOPK, INTER = 64, 8, 192
HALF_I = INTER // 2
TEAM = 4
TEAMS = EXP_N // TEAM
BLK = P // TEAM
RING = 3
LAPS = TEAMS // RING
EPS_LN, EPS_UNIT = 1e-5, 1e-6
XSCALE = float(1.0 / np.sqrt(np.float32(D)))
BIG = 1e30
LOWEST = -3.0e38


def perceiver(nc, x, ctxm, mask, w_qkv, w_out, q_gain, gate_w, gate_proj, up_proj, down_proj,
              rope_cs, out):
    es = ExitStack()
    with es:
        def sb(name, shape, dt=F32):
            return es.enter_context(nc.sbuf_tensor(name, shape, dt))

        def sem(name):
            return es.enter_context(nc.semaphore(name))

        psum = es.enter_context(nc.psum_tensor("psum", [P, 8, 512], F32))
        bank = [psum[:, i, :] for i in range(8)]

        ident = sb("ident", [P, P])
        ident_b = sb("ident_b", [P, P], BF16)
        causal_b = sb("causal_b", [P, 3, P], BF16)
        blk_c = sb("blk_c", [P, TH, 1])
        expert_row = sb("expert_row", [EXP_N, EXP_N])
        turn_row = sb("turn_row", [EXP_N, TEAMS // 2, 2, TEAM])
        slot_row = sb("slot_row", [P, BLK])
        ones_b = sb("ones_b", [P, P], BF16)
        ones_f = sb("ones_f", [P, HD])
        later_b = sb("later_b", [P, TH, TOK], BF16)
        col_i = sb("col_i", [P, 1])
        row8 = sb("row8", [NG, NG])

        x_sb = sb("x_sb", [P, TH, D])
        xn = sb("xn", [P, TH, D])
        xnT = sb("xnT", [P, DC, TOK])
        stats = sb("stats", [P, TH, 6])
        meanvar = sb("meanvar", [P, TH, 2])
        rstd = sb("rstd", [P, TH])
        var_eps = sb("var_eps", [P, TH])
        root_t = sb("root_t", [P, TH])

        mask_u8 = sb("mask_u8", [NG, GRP], U8)
        bias8 = sb("bias8", [NG, GRP])
        bias_g = sb("bias_g", [NG, GRP], BF16)
        flag = sb("flag", [NG, 1])
        flag_b = sb("flag_b", [NG, 1], BF16)
        col_b = sb("col_b", [EXP_N, 1], BF16)
        pick = sb("pick", [NG, NG])
        pick_b = sb("pick_b", [NG, NG], BF16)
        plan = sb("plan", [1, 16], I32)
        any_valid = sb("any_valid", [P, 1])

        GU_W = DC * INTER
        SLOT_W = 2 * GU_W + 2 * D
        weights01 = sb("weights01", [P, RING - 1, TEAM, SLOT_W])
        XA_W = 13 * 1024
        arena = weights01[:, :, :, :].rearrange("p r e n -> p (r e n)")
        off = [0]

        def carve(shape, dt=F32):
            n = int(np.prod(shape[1:])) * (4 if dt == F32 else 2) // 4
            assert off[0] + n <= arena.shape[1], (off, n)
            a = arena[:, off[0]:off[0] + n]
            off[0] += n
            if dt != F32:
                a = a.bitcast(dt)
            if len(shape) == 3:
                a = a.rearrange("p (a b) -> p a b", a=shape[1])
            if len(shape) == 4:
                a = a.rearrange("p (a b c) -> p a b c", a=shape[1], b=shape[2])
            if len(shape) == 5:
                a = a.rearrange("p (a b c d) -> p a b c d", a=shape[1], b=shape[2], c=shape[3])
            return a

        ctx_k = carve([P, KC, D])
        ctx_v = carve([P, 2, KC, D])
        ctxT = carve([P, DC, GRP])
        probs = carve([P, TH, GRP])
        probsT = carve([P, TH, KC, P])
        o_acc = carve([P, TH, D])
        m_run = sb("m_run", [P, TH])
        m_new = sb("m_new", [P, TH])
        m_grp = sb("m_grp", [P, TH])
        m_diff = sb("m_diff", [P, TH])
        nbias = sb("nbias", [P, TH])
        alpha = sb("alpha", [P, TH])
        r_sum = sb("r_sum", [P, TH])
        l_run = sb("l_run", [P, TH])
        o_scale = sb("o_scale", [P, TH])

        assert off[0] <= XA_W

        arena = sb("arena2", [P, 22016])[:, :]
        off[0] = 0
        wqkv_sb = carve([P, DC, 3 * D])
        wout_sb = carve([P, DC, D])
        qk_n = carve([P, TH, 2 * D])
        squares = carve([P, TH, 2 * D])
        rot = carve([P, 4, 256])
        v_sb = carve([P, TH, D])
        qkT = carve([P, HG, 2 * TOK])
        s_probs = carve([P, 2, 4, 3 * P])
        s_probsT = carve([P, 3, 4, P])
        y_inv = carve([P, TOK])
        off[0] = 0
        xparts = carve([P, TH, 3, DC, P], BF16)
        chosen = carve([P, TH, EXP_N])
        size_key = carve([P, 1])
        size_keys = carve([P, EXP_N])
        larger = carve([P, EXP_N])
        place = carve([P, 1])
        size_b = carve([P, 2], BF16)[:, 0:1]
        turn_b = carve([P, EXP_N], BF16)
        chosen_b = carve([P, TH, EXP_N], BF16)
        rexp = carve([P, TH, EXP_N])
        rw = carve([P, TH, EXP_N])
        rank = carve([P, TH, EXP_N])
        pick_t = carve([P, TH, TEAM, BLK], BF16)
        apart = carve([P, TH, TEAM, BLK])
        mix_t = carve([P, TH, TEAM, BLK])
        mixT = carve([P, TOK])
        xs = carve([P, DC, P])
        silu = carve([P, INTER])
        hid = carve([P, INTER])
        hidT = carve([P, 2, P])
        y_slot = carve([P, D])
        assert off[0] + TEAM * SLOT_W <= arena.shape[1]
        weights2 = arena[:, arena.shape[1] - TEAM * SLOT_W:].rearrange("p (e n) -> p e n", e=TEAM)
        ring = [weights01[:, 0], weights01[:, 1], weights2]

        cs_sb = sb("cs_sb", [P, TH, 2, HD // 2])
        gain_sb = sb("gain_sb", [P, HEADS])
        gate_sb = sb("gate_sb", [P, DC, EXP_N])
        head_ss = sb("head_ss", [P, TH, 2 * HEADS])
        head_r = sb("head_r", [P, TH, 2 * HEADS])
        head_t = sb("head_t", [P, TH, 2 * HEADS])
        s_max = sb("s_max", [P, 2, TH * 4])
        s_nmax = sb("s_nmax", [P, 2, TH * 4])
        logits = sb("logits", [P, TH, EXP_N])
        top8 = sb("top8", [P, TH, 8])
        cut = sb("cut", [P, TH, EXP_N])
        ntop = sb("ntop", [P, TH])
        rsum = sb("rsum", [P, TH])
        turns = sb("turns", [1, EXP_N], I32)
        cnt_i = sb("cnt_i", [1, TEAMS], I32)
        rounds = sb("rounds", [1, TEAMS], I32)

        s_x = sem("x_loaded")
        s_mask = sem("mask_loaded")
        s_const = sem("constants_ready")
        s_gpc = sem("gpsimd_chain")
        s_dve = sem("dve_chain")
        s_dvl = sem("dve_loop_chain")
        s_flag = sem("flags_ready")
        s_pos = sem("positions_ready")
        s_pick = sem("pick_ready")
        s_list = sem("list_in_psum")
        s_plan = sem("plan_ready")
        s_xn = sem("normed_ready")
        s_xnt = sem("normedT_in_psum")
        s_xnT = sem("normedT_ready")
        s_ck = sem("ctx_k_loaded")
        s_cv = sem("ctx_v_loaded")
        s_t = sem("ctxT_in_psum")
        s_ta = sem("ctxT_copied_act")
        s_td = sem("ctxT_copied_dve")
        s_bias = sem("bias_ready")
        s_s = sem("scores_ready")
        s_nb = sem("neg_max_ready")
        s_p = sem("probs_ready")
        s_al = sem("alpha_ready")
        s_pt = sem("probsT_in_psum")
        s_ptc = sem("probsT_ready")
        s_o = sem("readout_in_psum")
        s_oc = sem("readout_added")
        s_x1 = sem("x1_ready")
        s_out = sem("out_stored")
        s_tables = sem("tables_ready")
        s_small = sem("angles_and_gain_loaded")
        s_wq = sem("w_qkv_loaded")
        s_wo = sem("w_out_loaded")
        s_gw = sem("gate_w_loaded")
        s_qkv = sem("qkv_in_psum")
        s_sq = sem("squares_ready")
        s_v = sem("values_ready")
        s_rot = sem("rotated_ready")
        s_qkp = sem("qkT_in_psum")
        s_qka = sem("qkT_copied_act")
        s_qkd = sem("qkT_copied_dve")
        s_sc = sem("self_scores_ready")
        s_nm = sem("self_neg_max_ready")
        s_e = sem("self_probs_ready")
        s_spt = sem("self_probsT_in_psum")
        s_spa = sem("self_probsT_copied_act")
        s_spd = sem("self_probsT_copied_dve")
        s_pv = sem("self_values_in_psum")
        s_yn = sem("heads_normed")
        s_op = sem("projection_in_psum")
        s_x2 = sem("x2_ready")
        s_lg = sem("logits_in_psum")
        s_tv = sem("top_values_ready")
        s_ex = sem("router_exp_ready")
        s_ch = sem("chosen_ready")
        s_rw = sem("router_weights_ready")
        s_rank = sem("ranks_in_psum")
        s_xp1 = sem("first_parts_ready")
        s_xr1 = sem("first_rest_ready")
        s_xp2 = sem("second_parts_ready")
        s_xp = sem("third_parts_ready")
        s_trn = sem("turn_table_ready")
        s_lst = sem("turn_lists_in_psum")
        s_cnt = sem("turns_and_rounds_ready")
        s_rk = sem("rank_table_ready")
        s_ap = sem("rank_less_slot_ready")
        s_pk = sem("pick_written")
        s_gpr = sem("ranks_moved_on")
        s_mx = sem("mix_written")
        s_mtp = sem("mixT_in_psum")
        s_mt = sem("mixT_ready")
        s_xg = sem("gathered_in_psum")
        s_xgc = sem("gathered_ready")
        s_w = [sem(f"weights_loaded_{r}") for r in range(RING)]
        s_gu = sem("gate_up_in_psum")
        s_si = sem("silu_ready")
        s_h = sem("hidden_ready")
        s_htp = sem("hiddenT_in_psum")
        s_ht = sem("hiddenT_ready")
        s_y = sem("expert_out_in_psum")
        s_yc = sem("expert_out_copied")
        s_mm = sem("outputs_mixed")
        s_fin = sem("result_ready")

        block = es.enter_context(nc.Block())

        QK_BANKS = (6, 7, 0, 1)
        PT_BANKS = (6, 7, 0)

        class Chain:
            def __init__(self, eng, s, base=0):
                self.eng, self.s, self.base, self.n = eng, s, base, 0

            def step(self, ins, wait=True):
                self.n += 1
                ins.then_inc(self.s, 1)
                if wait:
                    self.wait()

            def wait(self):
                self.eng.wait_ge(self.s, self.base + self.n)

        ctx_rows = ctxm[0].rearrange("(g c p) d -> g p c d", g=NG, p=P)

        @block.sync
        def _(sp):
            sp.dma_start(mask_u8[:, :], mask[0].rearrange("(g n) -> g n", g=NG)).then_inc(s_mask, 16)
            sp.dma_start(x_sb[:, :, :], x[0].rearrange("(h p) d -> p h d", p=P)).then_inc(s_x, 16)
            sp.wait_ge(s_plan, 1)
            n = sp.value_load(plan[0:1, 15:16], min_val=1, max_val=NG)
            g = sp.value_load(plan[0:1, 0:1], min_val=0, max_val=NG - 1)
            sp.dma_start(ctx_k, ctx_rows[g]).then_inc(s_ck, 16)
            with sp.Fori(0, n) as i:
                gv = sp.value_load(plan[0:1, bass.ds(i, 1)], min_val=0, max_val=NG - 1)
                sp.wait_ge(s_oc, 2 * i + 1)
                sp.dma_start(ctx_v[:, bass.ds(i % 2, 1)], ctx_rows[gv]).then_inc(s_cv, 16)
                gk = sp.value_load(plan[0:1, bass.ds(i + 1, 1)], min_val=0, max_val=NG - 1)
                sp.wait_ge(s_t, DC * (i + 1))
                sp.dma_start(ctx_k, ctx_rows[gk]).then_inc(s_ck, 16)

            def team_of(q):
                return [sp.value_load(turns[0:1, bass.ds(q * TEAM + j, 1)], min_val=0, max_val=EXP_N - 1) for j in range(TEAM)]

            def load_team(team, r):
                for j, e in enumerate(team):
                    for dst, src in ((ring[r][:, j, 0:GU_W], gate_proj[bass.ds(e, 1)].rearrange("e (p c) n -> p (e c n)", c=DC)),
                                     (ring[r][:, j, GU_W:2 * GU_W], up_proj[bass.ds(e, 1)].rearrange("e (p c) n -> p (e c n)", c=DC)),
                                     (ring[r][0:HALF_I, j, 2 * GU_W:], down_proj[bass.ds(e, 1)].rearrange("e (p k) n -> p (e k n)", k=2))):
                        sp.dma_start(dst, src).then_inc(s_w[r], 16)

            sp.wait_ge(s_cnt, 2)
            for r in range(RING):
                load_team(team_of(r), r)
            done = sp.alloc_register("sp_done")
            sp.reg_mov(done, 0)

            def reload(q, r):
                count = sp.value_load(rounds[0:1, bass.ds(q - RING, 1)], min_val=1, max_val=TOK // BLK)
                sp.reg_add(done, done, count)
                team = team_of(q)
                sp.wait_ge(s_y, sp.snap(done))
                load_team(team, r)

            with sp.Fori(1, LAPS) as lap:
                for r in range(RING):
                    reload(lap * RING + r, r)
            reload(LAPS * RING, 0)
            for h in range(TH):
                sp.wait_ge(s_fin, h + 1)
                sp.dma_start(out[0, h * P:(h + 1) * P, :], x_sb[:, h]).then_inc(s_out, 16)
            sp.wait_ge(s_out, 32)

        @block.gpsimd
        def _(pool):
            ch = Chain(pool, s_gpc)
            ch.step(pool.memset(ident[:, :], 0.0), wait=False)
            ch.step(pool.memset(ones_b[:, :], 1.0), wait=False)
            ch.step(pool.memset(ident_b[:, :], 0.0), wait=False)
            ch.step(pool.memset(causal_b[:, :, :], 0.0), wait=False)
            ch.step(pool.memset(later_b[:, :, :], 1.0), wait=True)
            pool.affine_select(out=ident[:, :], in_=ident[:, :], compare_op=ALU.not_equal, fill=1.0,
                               base=0, pattern=[[-1, P]], channel_multiplier=1).then_inc(s_const, 1)
            pool.affine_select(out=later_b[:, :, :], in_=later_b[:, :, :], compare_op=ALU.is_gt, fill=0.0,
                               base=0, pattern=[[-P, TH], [1, TOK]], channel_multiplier=-1).then_inc(s_const, 1)
            pool.iota(col_i[:, :], pattern=[[0, 1]], base=0, channel_multiplier=1,
                      allow_small_or_imprecise_dtypes=True).then_inc(s_const, 1)
            pool.iota(row8[:, :], pattern=[[1, NG]], base=0, channel_multiplier=0,
                      allow_small_or_imprecise_dtypes=True).then_inc(s_const, 1)
            pool.affine_select(out=ident_b[:, :], in_=ident_b[:, :], compare_op=ALU.not_equal, fill=1.0,
                               base=0, pattern=[[-1, P]], channel_multiplier=1).then_inc(s_tables, 1)
            pool.affine_select(out=causal_b[:, 1:3, :], in_=causal_b[:, 1:3, :], compare_op=ALU.is_ge, fill=-BIG,
                               base=0, pattern=[[0, 2], [-1, P]], channel_multiplier=1).then_inc(s_tables, 1)
            pool.memset(ones_f[:, :], 1.0).then_inc(s_tables, 1)
            pool.memset(blk_c[:, :, :], float(BLK)).then_inc(s_tables, 1)
            pool.iota(expert_row[:, :], pattern=[[1, EXP_N]], base=0, channel_multiplier=0,
                      allow_small_or_imprecise_dtypes=True).then_inc(s_tables, 1)
            for k, (base, stride) in enumerate(((0, TEAM), (EXP_N - TEAM, -TEAM))):
                pool.iota(turn_row[:, :, k], pattern=[[stride, TEAMS // 2], [1, TEAM]], base=base, channel_multiplier=0,
                          allow_small_or_imprecise_dtypes=True).then_inc(s_tables, 1)
            pool.iota(slot_row[:, :], pattern=[[1, BLK]], base=0, channel_multiplier=0,
                      allow_small_or_imprecise_dtypes=True).then_inc(s_tables, 1)

            pool.wait_ge(s_tables, 8)
            pool.wait_ge(s_cnt, 2)
            pool.wait_ge(s_rk, 1)
            pool.wait_ge(s_rw, 1)
            step = pool.alloc_register("pool_step")
            pool.reg_mov(step, 0)
            slots = slot_row[:, :].unsqueeze(1).to_broadcast([P, TH, BLK])

            def over_slots(table, e):
                return table[:, :, bass.ds(e, 1)].to_broadcast([P, TH, BLK])

            with pool.Fori(0, TEAMS) as q:
                team = [pool.value_load(turns[0:1, bass.ds(q * TEAM + j, 1)], min_val=0, max_val=EXP_N - 1) for j in range(TEAM)]
                count = pool.value_load(rounds[0:1, bass.ds(q, 1)], min_val=1, max_val=TOK // BLK)
                with pool.Fori(0, count):
                    v = pool.snap(step)
                    pool.wait_ge(s_pk, v + 1)
                    pool.wait_ge(s_gpr, v + 1)
                    for j, e in enumerate(team):
                        last = pool.tensor_tensor(apart[:, :, j], over_slots(rank, e), slots, ALU.subtract)
                    last.then_inc(s_ap, 1)
                    pool.wait_ge(s_pk, v + 2)
                    pool.wait_ge(s_mtp, v + 1)
                    for j, e in enumerate(team):
                        last = pool.tensor_tensor(mix_t[:, :, j], pick_t[:, :, j], over_slots(rw, e), ALU.mult)
                    last.then_inc(s_mx, 1)
                    for j, e in enumerate(team):
                        left = rank[:, :, bass.ds(e, 1)]
                        last = pool.tensor_tensor(left, left, blk_c[:, :, :], ALU.subtract)
                    last.then_inc(s_gpr, 1)
                    pool.reg_add(step, step, 1)
            pool.wait_ge(s_pk, pool.snap(step) + 1)
            pool.tensor_tensor(apart, apart, apart, ALU.subtract).then_inc(s_ap, 1)

        def inverse_root(dve, ch, y, v, t):
            yi, vi = y.bitcast(I32), v.bitcast(I32)
            ch.step(dve.tensor_scalar(yi, vi, 1, None, ALU.logical_shift_right))
            ch.step(dve.tensor_scalar(yi, yi, -1.0, float(0x5F3759DF), ALU.mult, ALU.add))
            for _ in range(3):
                ch.step(dve.tensor_tensor(t, y, y, ALU.mult))
                ch.step(dve.scalar_tensor_tensor(t, t, -0.5, v, ALU.mult, ALU.mult))
                ch.step(dve.scalar_tensor_tensor(y, t, 1.5, y, ALU.add, ALU.mult))

        def layer_norm(dve, ch):
            for h in range(TH):
                ch.step(dve.bn_stats(stats[:, h, :], x_sb[:, h, :]), wait=False)
            ch.wait()
            for h in range(TH):
                ch.step(dve.bn_aggr(meanvar[:, h, :], stats[:, h, :]), wait=False)
            ch.wait()
            ch.step(dve.tensor_scalar(var_eps[:, :], meanvar[:, :, 1], EPS_LN, None, ALU.add))
            inverse_root(dve, ch, rstd[:, :], var_eps[:, :], root_t[:, :])
            for h in range(TH):
                dve.tensor_scalar(xn[:, h, :], x_sb[:, h, :], meanvar[:, h, 0:1], rstd[:, h:h + 1],
                                  ALU.subtract, ALU.mult).then_inc(s_xn, 1)

        def transpose_xn(pe, banks):
            for c in range(DC):
                for h in range(TH):
                    last = pe.transpose(banks[c // 2][:, (c % 2) * TOK + h * P:(c % 2) * TOK + (h + 1) * P],
                                        xn[:, h, c::DC], ident[:, :])
                if c % 2:
                    last.then_inc(s_xnt, 1)

        def copy_xnT(dve, done, b):
            for j in range(2):
                dve.wait_ge(s_xnt, done + j + 1)
                dve.tensor_copy(xnT[:, 2 * j:2 * j + 2, :],
                                bank[b + j].rearrange("p (c t) -> p c t", c=2)).then_inc(s_xnT, 1)

        @block.vector
        def _(dve):
            ch = Chain(dve, s_dve)
            for h in range(TH):
                dve.memset(o_acc[:, h], 0.0).then_inc(s_oc, 1)
            dve.memset(alpha[:, :], 0.0).then_inc(s_oc, 1)
            ch.step(dve.memset(l_run[:, :], 0.0), wait=False)
            ch.step(dve.memset(m_run[:, :], LOWEST), wait=False)
            dve.wait_ge(s_const, 4)
            ch.step(dve.tensor_copy(col_b[:, :], col_i[0:EXP_N, :]), wait=False)
            dve.wait_ge(s_mask, 16)
            ch.step(dve.tensor_reduce(flag[:, :], mask_u8[:, :], AX.X, ALU.max))
            dve.tensor_copy(flag_b[:, :], flag[:, :]).then_inc(s_flag, 1)
            ch.step(dve.tensor_scalar(bias8[:, :], mask_u8[:, :], 1.0, BIG, ALU.subtract, ALU.mult))
            dve.wait_ge(s_pos, 1)
            ch.step(dve.tensor_scalar(pick[:, :], row8[:, :], bank[7][0:NG, 0:1], flag[:, :],
                                      ALU.is_equal, ALU.mult))
            dve.tensor_copy(pick_b[:, :], pick[:, :]).then_inc(s_pick, 1)
            ch.step(dve.tensor_scalar(any_valid[:, :], bank[7][:, 1:2], 1.0, None, ALU.min), wait=False)
            ch.step(dve.memset(plan[:, :], 0))
            dve.wait_ge(s_list, 1)
            ch.step(dve.tensor_copy(plan[0:1, 0:NG], bank[6][0:1, 0:NG]), wait=False)
            dve.tensor_scalar(plan[0:1, 15:16], bank[7][0:1, 1:2], 1.0, None, ALU.max).then_inc(s_plan, 1)
            dve.wait_ge(s_x, 16)
            layer_norm(dve, ch)
            copy_xnT(dve, 0, 4)

            def copy_ctxT(k):
                for c in (2, 3):
                    dve.wait_ge(s_t, DC * k + c + 1)
                    dve.tensor_copy(ctxT[:, c, :], bank[c][:, :]).then_inc(s_td, 1)

            dve.wait_ge(s_plan, 1)
            n = dve.value_load(plan[0:1, 15:16], min_val=1, max_val=NG)
            copy_ctxT(0)
            STEPS = 10
            with dve.Fori(0, n) as i:
                lc = Chain(dve, s_dvl, base=i * STEPS)
                dve.tensor_scalar(bias_g[:, :], bias8[:, :], pick[:, bass.ds(i, 1)], None, ALU.mult).then_inc(s_bias, 1)
                for h in range(TH):
                    hs = slice(h, h + 1)
                    dve.wait_ge(s_s, 2 * i + h + 1)
                    lc.step(dve.tensor_reduce(m_grp[:, hs], bank[4 + h][:, :], AX.X, ALU.max))
                    lc.step(dve.tensor_tensor(m_new[:, hs], m_run[:, hs], m_grp[:, hs], ALU.max))
                    lc.step(dve.tensor_tensor(m_diff[:, hs], m_run[:, hs], m_new[:, hs], ALU.subtract), wait=False)
                    dve.tensor_scalar(nbias[:, hs], m_new[:, hs], -XSCALE, None, ALU.mult).then_inc(s_nb, 1)
                    lc.wait()
                    lc.step(dve.tensor_copy(m_run[:, hs], m_new[:, hs]), wait=False)
                copy_ctxT(i + 1)
                for h in range(TH):
                    dve.wait_ge(s_pt, 2 * i + h + 1)
                    dve.tensor_copy(probsT[:, h], bank[6 + h][:, :].rearrange("p (k t) -> p k t", k=KC)).then_inc(s_ptc, 1)
                for h in range(TH):
                    hs = slice(h, h + 1)
                    dve.wait_ge(s_al, 2 * i + h + 1)
                    dve.wait_ge(s_p, 2 * i + h + 1)
                    lc.step(dve.scalar_tensor_tensor(l_run[:, hs], l_run[:, hs], alpha[:, hs], r_sum[:, hs],
                                                     ALU.mult, ALU.add), wait=False)
                    dve.wait_ge(s_o, 2 * i + h + 1)
                    dve.scalar_tensor_tensor(o_acc[:, h], o_acc[:, h], alpha[:, hs], bank[4 + h][:, :],
                                             ALU.mult, ALU.add).then_inc(s_oc, 1)
                lc.wait()
                assert lc.n == STEPS, lc.n
            dve.wait_ge(s_oc, 2 * n + 3)
            dve.wait_ge(s_ta, 2 * n + 2)
            ch.step(dve.reciprocal(o_scale[:, :], l_run[:, :]))
            ch.step(dve.tensor_scalar(o_scale[:, :], o_scale[:, :], any_valid[:, :], None, ALU.mult))
            for h in range(TH):
                dve.scalar_tensor_tensor(x_sb[:, h], o_acc[:, h], o_scale[:, h:h + 1], x_sb[:, h],
                                         ALU.mult, ALU.add).then_inc(s_x1, 1)

            dve.wait_ge(s_x1, 2)
            layer_norm(dve, ch)
            copy_xnT(dve, 2, 6)
            dve.wait_ge(s_small, 32)
            for h in range(TH):
                dve.wait_ge(s_sq, 2 * h + 2)
                ch.step(dve.tensor_reduce(head_ss[:, h], squares[:, h].rearrange("p (a d) -> p a d", d=HD), AX.X, ALU.add))
                ch.step(dve.tensor_scalar(head_ss[:, h], head_ss[:, h], EPS_UNIT, None, ALU.add))
                inverse_root(dve, ch, head_r[:, h], head_ss[:, h], head_t[:, h])
                ch.step(dve.tensor_tensor(head_r[:, h, 0:HEADS], head_r[:, h, 0:HEADS], gain_sb[:, :], ALU.mult))
                for j in range(2):
                    ch.step(dve.tensor_tensor(
                        qk_n[:, h, j * D:(j + 1) * D].rearrange("p (a d) -> p a d", d=HD),
                        bank[3 * h + j].rearrange("p (a d) -> p a d", d=HD),
                        head_r[:, h, j * HEADS:(j + 1) * HEADS].unsqueeze(2).to_broadcast([P, HEADS, HD]),
                        ALU.mult), wait=False)
                ch.wait()
                even = qk_n[:, h].rearrange("p (a d) -> p a d", d=2 * HD)
                t1, t2 = even[:, :, 0:HD // 2], even[:, :, HD // 2:HD]
                cos = cs_sb[:, h, 0, :].unsqueeze(1).to_broadcast([P, HEADS, HD // 2])
                sin = cs_sb[:, h, 1, :].unsqueeze(1).to_broadcast([P, HEADS, HD // 2])
                parts = [rot[:, n].rearrange("p (a d) -> p a d", d=HD // 2) for n in range(4)]
                for dst, t, f in zip(parts, (t1, t2, t1, t2), (cos, sin, sin, cos)):
                    ch.step(dve.tensor_tensor(dst, t, f, ALU.mult), wait=False)
                ch.wait()
                ch.step(dve.tensor_tensor(t1, parts[0], parts[1], ALU.subtract), wait=False)
                dve.tensor_tensor(t2, parts[2], parts[3], ALU.add).then_inc(s_rot, 1)
                ch.wait()
            for g in (1, 3):
                dve.wait_ge(s_qkp, g + 1)
                dve.tensor_copy(qkT[:, g, :], bank[QK_BANKS[g]]).then_inc(s_qkd, 1)

            def row_max(g):
                b = g % 2
                dve.wait_ge(s_sc, 4 * g + 4)
                ch.step(dve.tensor_reduce(s_max[:, b, 4:8], psum[:, 2:6, 0:2 * P], AX.X, ALU.max), wait=False)
                ch.step(dve.tensor_reduce(s_max[:, b, 0:4], psum[:, 2:6, 2 * P:3 * P], AX.X, ALU.max))
                dve.tensor_scalar(s_nmax[:, b, :], s_max[:, b, :], -1.0, None, ALU.mult).then_inc(s_nm, 1)

            row_max(0)
            for g in range(HG):
                if g:
                    dve.wait_ge(s_pv, g)
                for j in (1, 2):
                    dve.wait_ge(s_spt, 3 * g + j + 1)
                    dve.tensor_copy(s_probsT[:, j], bank[PT_BANKS[j]].rearrange("p (r t) -> p r t", r=4)).then_inc(s_spd, 1)
                if g + 1 < HG:
                    row_max(g + 1)
                dve.wait_ge(s_pv, g + 1)
                ch.step(dve.reciprocal(y_inv, bank[1][:, TOK:2 * TOK]))
                dve.tensor_tensor(xnT[:, g, :], bank[1][:, 0:TOK], y_inv, ALU.mult).then_inc(s_yn, 1)
            for h in range(TH):
                dve.wait_ge(s_op, h + 1)
                dve.tensor_tensor(x_sb[:, h], x_sb[:, h], bank[4 + h], ALU.add).then_inc(s_x2, 1)

            dve.wait_ge(s_x2, 2)
            layer_norm(dve, ch)
            copy_xnT(dve, 4, 6)
            rest = xn
            dve.wait_ge(s_xp1, 2)
            for h in range(TH):
                dve.tensor_tensor(rest[:, h].rearrange("p (q c) -> p c q", c=DC), xn[:, h].rearrange("p (q c) -> p c q", c=DC),
                                  xparts[:, h, 0], ALU.subtract).then_inc(s_xr1, 1)
            dve.wait_ge(s_lg, 1)
            ch.step(dve.tensor_copy(logits[:, :, :], bank[0][:, 0:TH * EXP_N].rearrange("p (h e) -> p h e", h=TH)))
            for h in range(TH):
                ch.step(dve.max(top8[:, h], logits[:, h]), wait=False)
            ch.wait()
            dve.tensor_scalar(ntop[:, :], top8[:, :, 0], -1.0, None, ALU.mult).then_inc(s_tv, 1)
            for h in range(TH):
                ch.step(dve.match_replace(cut[:, h], top8[:, h], logits[:, h], LOWEST), wait=False)
            ch.wait()
            ch.step(dve.tensor_tensor(chosen, cut[:, :, :], logits[:, :, :], ALU.not_equal))
            dve.tensor_copy(chosen_b, chosen).then_inc(s_ch, 1)
            dve.wait_ge(s_tables, 8)
            dve.wait_ge(s_rank, 1)
            n_col, n_row = bank[2][0:EXP_N, 0:1], bank[2][0:EXP_N, EXP_N:2 * EXP_N]
            ch.step(dve.tensor_scalar(size_key[0:EXP_N], n_col, float(EXP_N), col_i[0:EXP_N, :], ALU.mult, ALU.subtract), wait=False)
            ch.step(dve.scalar_tensor_tensor(size_keys[0:EXP_N], n_row, float(EXP_N), expert_row[:, :], ALU.mult, ALU.subtract), wait=False)
            ch.step(dve.tensor_copy(size_b[0:EXP_N], n_col))
            ch.step(dve.tensor_scalar(larger[0:EXP_N], size_keys[0:EXP_N], size_key[0:EXP_N], None, ALU.is_gt))
            ch.step(dve.tensor_reduce(place[0:EXP_N], larger[0:EXP_N], AX.X, ALU.add))
            dve.tensor_scalar(turn_b[0:EXP_N], turn_row[:, :, :, :].rearrange("p a b c -> p (a b c)"), place[0:EXP_N],
                              None, ALU.is_equal).then_inc(s_trn, 1)
            ch.step(dve.scalar_tensor_tensor(rank, bank[1][:, 0:TH * EXP_N].rearrange("p (h e) -> p h e", h=TH), 1.0,
                                             chosen, ALU.add, ALU.mult))
            dve.tensor_scalar(rank, rank, 1.0, None, ALU.subtract).then_inc(s_rk, 1)
            dve.wait_ge(s_lst, 1)
            dve.tensor_copy(turns[:, :], bank[3][0:1, 0:EXP_N]).then_inc(s_cnt, 1)
            ch.step(dve.tensor_reduce(cnt_i[:, :], bank[3][0:1, EXP_N:2 * EXP_N].rearrange("p (q e) -> p q e", e=TEAM), AX.X, ALU.max))
            ch.step(dve.tensor_scalar(cnt_i[:, :], cnt_i[:, :], float(BLK - 1), None, ALU.add))
            ch.step(dve.tensor_scalar(cnt_i[:, :], cnt_i[:, :], BLK.bit_length() - 1, None, ALU.arith_shift_right))
            dve.tensor_scalar(rounds[:, :], cnt_i[:, :], 1.0, None, ALU.max).then_inc(s_cnt, 1)
            dve.memset(mixT, 0.0).then_inc(s_mt, 1)
            dve.memset(y_slot, 0.0).then_inc(s_yc, 1)
            dve.memset(pick_t, 0.0).then_inc(s_pk, 1)
            dve.memset(mix_t, 0.0).then_inc(s_mtp, 1)
            dve.memset(hidT, 0.0).then_inc(s_gpr, 1)
            dve.wait_ge(s_xp2, 2)
            for h in range(TH):
                dve.tensor_tensor(xparts[:, h, 2], rest[:, h].rearrange("p (q c) -> p c q", c=DC),
                                  xparts[:, h, 1], ALU.subtract).then_inc(s_xp, 1)
            dve.wait_ge(s_ex, 2)
            ch.step(dve.tensor_tensor(rexp, rexp, chosen, ALU.mult))
            ch.step(dve.tensor_reduce(rsum[:, :], rexp, AX.X, ALU.add))
            ch.step(dve.reciprocal(rsum[:, :], rsum[:, :]))
            dve.tensor_tensor(rw, rexp, rsum[:, :].unsqueeze(2).to_broadcast([P, TH, EXP_N]), ALU.mult).then_inc(s_rw, 1)

            def write_pick():
                dve.tensor_scalar(pick_t, apart, 0.0, None, ALU.is_equal).then_inc(s_pk, 1)

            dve.wait_ge(s_pk, 1)
            dve.wait_ge(s_ap, 1)
            write_pick()
            step = dve.alloc_register("dve_step")
            dve.reg_mov(step, 0)
            with dve.Fori(0, TEAMS) as q:
                count = dve.value_load(rounds[0:1, bass.ds(q, 1)], min_val=1, max_val=TOK // BLK)
                with dve.Fori(0, count):
                    v = dve.snap(step)
                    dve.wait_ge(s_ap, v + 2)
                    dve.wait_ge(s_xg, v + 1)
                    dve.wait_ge(s_mx, v + 1)
                    write_pick()
                    dve.wait_ge(s_si, v + 1)
                    dve.tensor_tensor(hid, silu, bank[0][:, INTER:2 * INTER], ALU.mult).then_inc(s_h, 1)
                    dve.wait_ge(s_htp, v + 1)
                    dve.tensor_copy(hidT[0:HALF_I], bank[1][0:HALF_I, 0:2 * P].rearrange("p (k s) -> p k s", k=2)).then_inc(s_ht, 1)
                    dve.wait_ge(s_mtp, v + 2)
                    dve.wait_ge(s_y, v + 1)
                    dve.tensor_copy(mixT, bank[2][:, 0:TOK]).then_inc(s_mt, 1)
                    dve.reg_add(step, step, 1)

            for h in range(TH):
                dve.wait_ge(s_mm, h + 1)
                dve.tensor_tensor(x_sb[:, h], x_sb[:, h], bank[4 + h], ALU.add).then_inc(s_fin, 1)

        @block.scalar
        def _(act):
            act.dma_start(cs_sb[:, :, :, :], rope_cs.rearrange("(h p) a d -> p h a d", p=P)).then_inc(s_small, 16)
            act.dma_start(gain_sb[:, :], q_gain.partition_broadcast(P)).then_inc(s_small, 16)
            act.wait_ge(s_plan, 1)
            n = act.value_load(plan[0:1, 15:16], min_val=1, max_val=NG)

            def copy_ctxT(k):
                for c in (0, 1):
                    act.wait_ge(s_t, DC * k + c + 1)
                    act.activation(ctxT[:, c, :], bank[c][:, :], ACT.Copy).then_inc(s_ta, 1)

            copy_ctxT(0)
            act.dma_start(wqkv_sb, w_qkv.rearrange("(p c) n -> p c n", c=DC)).then_inc(s_wq, 16)
            act.dma_start(wout_sb, w_out.rearrange("(c p) n -> p c n", c=DC)).then_inc(s_wo, 16)
            act.dma_start(gate_sb[:, :, :], gate_w.rearrange("(p c) n -> p c n", c=DC)).then_inc(s_gw, 16)
            with act.Fori(0, n) as i:
                for h in range(TH):
                    act.wait_ge(s_nb, 2 * i + h + 1)
                    act.activation(probs[:, h], bank[4 + h][:, :], ACT.Exp, bias=nbias[:, h:h + 1], scale=XSCALE,
                                   accum_out=r_sum[:, h:h + 1]).then_inc(s_p, 1)
                    act.activation(alpha[:, h:h + 1], m_diff[:, h:h + 1], ACT.Exp, scale=XSCALE).then_inc(s_al, 1)
                copy_ctxT(i + 1)

            for h in range(TH):
                for j in range(2):
                    act.wait_ge(s_qkv, 3 * h + j + 1)
                    act.activation(squares[:, h, j * D:(j + 1) * D], bank[3 * h + j], ACT.Square).then_inc(s_sq, 1)
                act.wait_ge(s_qkv, 3 * h + 3)
                act.activation(v_sb[:, h], bank[3 * h + 2], ACT.Copy).then_inc(s_v, 1)
            for g in (0, 2):
                act.wait_ge(s_qkp, g + 1)
                act.activation(qkT[:, g, :], bank[QK_BANKS[g]], ACT.Copy).then_inc(s_qka, 1)

            def self_exp(g):
                b = g % 2
                act.wait_ge(s_nm, g + 1)
                if g >= 2:
                    act.wait_ge(s_spt, 3 * (g - 1))
                for r in range(4):
                    act.activation(s_probs[:, b, r, 0:2 * P], bank[2 + r][:, 0:2 * P], ACT.Exp,
                                   bias=s_nmax[:, b, 4 + r:5 + r]).then_inc(s_e, 1)
                    act.activation(s_probs[:, b, r, 2 * P:3 * P], bank[2 + r][:, 2 * P:3 * P], ACT.Exp,
                                   bias=s_nmax[:, b, r:r + 1]).then_inc(s_e, 1)

            self_exp(0)
            for g in range(HG):
                if g:
                    act.wait_ge(s_pv, g)
                act.wait_ge(s_spt, 3 * g + 1)
                act.activation(s_probsT[:, 0], bank[PT_BANKS[0]].rearrange("p (r t) -> p r t", r=4), ACT.Copy).then_inc(s_spa, 1)
                if g + 1 < HG:
                    self_exp(g + 1)

            for h in range(TH):
                act.wait_ge(s_xn, 4 + h + 1)
                act.activation(xparts[:, h, 0], xn[:, h].rearrange("p (q c) -> p c q", c=DC), ACT.Copy).then_inc(s_xp1, 1)
            for h in range(TH):
                act.wait_ge(s_xr1, h + 1)
                act.activation(xparts[:, h, 1], xn[:, h].rearrange("p (q c) -> p c q", c=DC), ACT.Copy).then_inc(s_xp2, 1)
            act.wait_ge(s_tv, 1)
            for h in range(TH):
                act.activation(rexp[:, h], logits[:, h], ACT.Exp, bias=ntop[:, h:h + 1]).then_inc(s_ex, 1)

            def copy_gathered():
                act.activation(xs, bank[3].rearrange("p (c s) -> p c s", c=DC), ACT.Copy).then_inc(s_xgc, 1)

            act.wait_ge(s_cnt, 2)
            act.wait_ge(s_xg, 1)
            copy_gathered()
            step = act.alloc_register("act_step")
            act.reg_mov(step, 0)
            with act.Fori(0, TEAMS) as q:
                count = act.value_load(rounds[0:1, bass.ds(q, 1)], min_val=1, max_val=TOK // BLK)
                with act.Fori(0, count):
                    v = act.snap(step)
                    act.wait_ge(s_gu, v + 1)
                    act.activation(silu, bank[0][:, 0:INTER], ACT.Silu).then_inc(s_si, 1)
                    act.wait_ge(s_xg, v + 2)
                    copy_gathered()
                    act.wait_ge(s_y, v + 1)
                    act.activation(y_slot, bank[6], ACT.Copy).then_inc(s_yc, 1)
                    act.reg_add(step, step, 1)

        @block.tensor
        def _(pe):
            pe.wait_ge(s_const, 4)
            pe.wait_ge(s_flag, 1)
            pe.matmul(bank[7][0:NG, 0:1], later_b[0:NG, 0, 0:NG], flag_b[:, :], start=True, stop=True)
            pe.matmul(bank[7][:, 1:2], ones_b[0:NG, :], flag_b[:, :], start=True, stop=True).then_inc(s_pos, 1)
            pe.wait_ge(s_pick, 1)
            pe.matmul(bank[6][0:1, 0:NG], col_b[0:NG, :], pick_b[:, :], start=True, stop=True).then_inc(s_list, 1)
            pe.wait_ge(s_xn, 2)
            transpose_xn(pe, bank[4:6])
            pe.wait_ge(s_plan, 1)
            n = pe.value_load(plan[0:1, 15:16], min_val=1, max_val=NG)

            def transpose_ctx():
                for c in range(DC):
                    for k in range(KC):
                        last = pe.transpose(bank[c][:, k * P:(k + 1) * P], ctx_k[:, k, c::DC], ident[:, :])
                    last.then_inc(s_t, 1)

            pe.wait_ge(s_ck, 16)
            transpose_ctx()
            pe.wait_ge(s_xnT, 2)
            with pe.Fori(0, n) as i:
                pe.wait_ge(s_bias, i + 1)
                pe.wait_ge(s_ta, 2 * i + 2)
                pe.wait_ge(s_td, 2 * i + 2)
                for h in range(TH):
                    pe.wait_ge(s_oc, 2 * i + h + 2)
                    pe.matmul(bank[4 + h][:, :], ones_b[0:NG, :], bias_g[:, :], start=True, stop=False)
                    for c in range(DC):
                        last = pe.matmul(bank[4 + h][:, :], xnT[:, c, h * P:(h + 1) * P], ctxT[:, c, :],
                                         start=False, stop=(c == DC - 1))
                    last.then_inc(s_s, 1)
                pe.wait_ge(s_ck, 16 * (i + 2))
                transpose_ctx()
                for h in range(TH):
                    pe.wait_ge(s_p, 2 * i + h + 1)
                    for k in range(KC):
                        last = pe.transpose(bank[6 + h][:, k * P:(k + 1) * P], probs[:, h, k * P:(k + 1) * P], ident[:, :])
                    last.then_inc(s_pt, 1)
                pe.wait_ge(s_cv, 16 * (i + 1))
                for h in range(TH):
                    pe.wait_ge(s_ptc, 2 * i + h + 1)
                    for k in range(KC):
                        last = pe.matmul(bank[4 + h][:, :], probsT[:, h, k, :], ctx_v[:, bass.ds(i % 2, 1), k, :],
                                         start=(k == 0), stop=(k == KC - 1))
                    last.then_inc(s_o, 1)

            pe.wait_ge(s_tables, 3)
            pe.wait_ge(s_ta, 2 * n + 2)
            pe.wait_ge(s_xn, 4)
            transpose_xn(pe, bank[6:8])
            pe.wait_ge(s_xnT, 4)
            pe.wait_ge(s_wq, 16)
            for h in range(TH):
                for j in range(3):
                    for c in range(DC):
                        last = pe.matmul(bank[3 * h + j], xnT[:, c, h * P:(h + 1) * P], wqkv_sb[:, c, j * D:(j + 1) * D],
                                         start=(c == 0), stop=(c == DC - 1))
                    last.then_inc(s_qkv, 1)
            for h in range(TH):
                pe.wait_ge(s_rot, h + 1)
                for g in range(HG):
                    for j in range(2):
                        last = pe.transpose(bank[QK_BANKS[g]][:, j * TOK + h * P:j * TOK + (h + 1) * P],
                                            qk_n[:, h, j * D + g * P:j * D + (g + 1) * P], ident[:, :])
                    if h:
                        last.then_inc(s_qkp, 1)
            pe.wait_ge(s_v, 2)

            def self_scores(g):
                if g % 2 == 0:
                    pe.wait_ge(s_qka, g // 2 + 1)
                else:
                    pe.wait_ge(s_qkd, g // 2 + 1)
                for r in range(4):
                    if g:
                        pe.wait_ge(s_e, 8 * (g - 1) + 2 * r + 2)
                    rows = slice(HD * r, HD * (r + 1))
                    pe.matmul(bank[2 + r][:, 0:3 * P], ident_b[:, :], causal_b[:, :, :], start=True, stop=False)
                    pe.matmul(bank[2 + r][:, 0:2 * P], qkT[rows, g, P:2 * P], qkT[rows, g, TOK:TOK + 2 * P],
                              start=False, stop=False)
                    pe.matmul(bank[2 + r][:, 2 * P:3 * P], qkT[rows, g, 0:P], qkT[rows, g, TOK:TOK + P],
                              start=False, stop=True).then_inc(s_sc, 1)

            self_scores(0)
            pe.wait_ge(s_qka, 2)
            pe.wait_ge(s_qkd, 2)
            for g in range(HG):
                if g:
                    pe.wait_ge(s_spa, g)
                    pe.wait_ge(s_spd, 2 * g)
                for r in range(4):
                    pe.wait_ge(s_e, 8 * g + 2 * r + 2)
                    for j in range(3):
                        last = pe.transpose(bank[PT_BANKS[j]][:, r * P:(r + 1) * P],
                                            s_probs[:, g % 2, r, j * P:(j + 1) * P], ident[:, :])
                        if r == 3:
                            last.then_inc(s_spt, 1)
                if g + 1 < HG:
                    self_scores(g + 1)
                pe.wait_ge(s_spa, g + 1)
                pe.wait_ge(s_spd, 2 * g + 2)
                if g:
                    pe.wait_ge(s_yn, g)
                for at, left in ((0, lambda k, head: v_sb[:, k, head]), (TOK, lambda k, head: ones_f[:, :])):
                    for dst, j, k in ((0, 2, 0), (P, 0, 0), (P, 1, 1)):
                        for r in range(4):
                            head = slice((4 * g + r) * HD, (4 * g + r + 1) * HD)
                            last = pe.matmul(bank[1][r * HD:(r + 1) * HD, at + dst:at + dst + P], left(k, head),
                                             s_probsT[:, j, r, :], start=(k == 0), stop=(j != 0))
                last.then_inc(s_pv, 1)
            pe.wait_ge(s_yn, HG)
            pe.wait_ge(s_wo, 16)
            for h in range(TH):
                for c in range(DC):
                    last = pe.matmul(bank[4 + h], xnT[:, c, h * P:(h + 1) * P], wout_sb[:, c, :],
                                     start=(c == 0), stop=(c == DC - 1))
                last.then_inc(s_op, 1)

            pe.wait_ge(s_xn, 6)
            transpose_xn(pe, bank[6:8])
            pe.wait_ge(s_xnT, 6)
            pe.wait_ge(s_gw, 16)
            for h in range(TH):
                for c in range(DC):
                    last = pe.matmul(bank[0][:, h * EXP_N:(h + 1) * EXP_N], xnT[:, c, h * P:(h + 1) * P], gate_sb[:, c, :],
                                     start=(c == 0), stop=(c == DC - 1))
            last.then_inc(s_lg, 1)
            pe.wait_ge(s_ch, 1)
            for q in range(TH):
                for h in range(q + 1):
                    pe.matmul(bank[1][:, q * EXP_N:(q + 1) * EXP_N], later_b[:, h, q * P:(q + 1) * P], chosen_b[:, h],
                              start=(h == 0), stop=(h == q))
            for dst, left, right in ((bank[2][0:EXP_N, EXP_N:2 * EXP_N], lambda h: ones_b[:, 0:EXP_N], lambda h: chosen_b[:, h]),
                                     (bank[2][0:EXP_N, 0:1], lambda h: chosen_b[:, h], lambda h: ones_b[:, 0:1])):
                for h in range(TH):
                    last = pe.matmul(dst, left(h), right(h), start=(h == 0), stop=(h == TH - 1))
            last.then_inc(s_rank, 1)
            pe.wait_ge(s_trn, 1)
            pe.matmul(bank[3][0:1, 0:EXP_N], col_b[:, :], turn_b[0:EXP_N], start=True, stop=True)
            pe.matmul(bank[3][0:1, EXP_N:2 * EXP_N], size_b[0:EXP_N], turn_b[0:EXP_N], start=True, stop=True).then_inc(s_lst, 1)

            def gather():
                for c in range(DC):
                    for k, (part, h) in enumerate((part, h) for part in range(3) for h in range(TH)):
                        last = pe.matmul(bank[3][:, c * P:(c + 1) * P], xparts[:, h, part, c, :], pick_t[:, h],
                                         start=(k == 0), stop=(k == 3 * TH - 1))
                last.then_inc(s_xg, 1)

            def mix(start=False, stop=False):
                for h in range(TH):
                    last = pe.matmul(bank[4 + h], mixT[:, h * P:(h + 1) * P], y_slot, start=start, stop=stop)
                    if stop:
                        last.then_inc(s_mm, 1)

            pe.wait_ge(s_cnt, 2)
            pe.wait_ge(s_mt, 1)
            pe.wait_ge(s_yc, 1)
            mix(start=True)
            pe.wait_ge(s_xp, 2)
            pe.wait_ge(s_pk, 2)
            gather()
            step = pe.alloc_register("pe_step")
            pe.reg_mov(step, 0)
            def team_rounds(q, r, loads):
                pe.wait_ge(s_w[r], 16 * 3 * TEAM * loads)
                count = pe.value_load(rounds[0:1, bass.ds(q, 1)], min_val=1, max_val=TOK // BLK)
                with pe.Fori(0, count):
                    v = pe.snap(step)
                    pe.wait_ge(s_xgc, v + 1)
                    for c in range(DC):
                        for e in range(TEAM):
                            quarter = slice(e * BLK, (e + 1) * BLK)
                            w = ring[r][:, e, 0:2 * GU_W].rearrange("p (g c n) -> p g c n", g=2, c=DC)
                            last = pe.matmul(bank[0][quarter, 0:2 * INTER], xs[:, c, quarter], w[:, :, c, :],
                                             start=(c == 0), stop=(c == DC - 1))
                    last.then_inc(s_gu, 1)
                    pe.wait_ge(s_pk, v + 3)
                    gather()
                    pe.wait_ge(s_mx, v + 1)
                    pe.wait_ge(s_mt, v + 1)
                    for h in range(TH):
                        last = pe.transpose(bank[2][:, h * P:(h + 1) * P], mix_t[:, h].rearrange("p e s -> p (e s)"), ident[:, :])
                    last.then_inc(s_mtp, 1)
                    pe.wait_ge(s_h, v + 1)
                    for k in range(2):
                        last = pe.transpose(bank[1][0:HALF_I, k * P:(k + 1) * P], hid[:, k::2], ident[:, :])
                    last.then_inc(s_htp, 1)
                    pe.wait_ge(s_yc, v + 1)
                    mix()
                    pe.wait_ge(s_ht, v + 1)
                    for k in range(2):
                        for e in range(TEAM):
                            quarter = slice(e * BLK, (e + 1) * BLK)
                            last = pe.matmul(bank[6][quarter, :], hidT[0:HALF_I, k, quarter],
                                             ring[r][0:HALF_I, e, 2 * GU_W + k * D:2 * GU_W + (k + 1) * D],
                                             start=(k == 0), stop=(k == 1))
                    last.then_inc(s_y, 1)
                    pe.reg_add(step, step, 1)

            with pe.Fori(0, LAPS) as lap:
                for r in range(RING):
                    team_rounds(lap * RING + r, r, lap + 1)
            team_rounds(LAPS * RING, 0, LAPS + 1)
            pe.wait_ge(s_yc, pe.snap(step) + 1)
            pe.wait_ge(s_mt, pe.snap(step) + 1)
            mix(stop=True)


_INS = ['x', 'ctx_2048', 'mask_BxS2_bk0', 'L0_attn_w_qkv', 'L0_attn_w_out', 'L0_attn_q_gain', 'L0_ffn_gate_w',
        'L0_ffn_gate_proj_w', 'L0_ffn_up_proj_w', 'L0_ffn_down_proj_w']


def kernel(**inputs):
    import numpy as _np
    import concourse.bacc as _bacc
    from concourse import mybir as _mybir
    from concourse.bass_utils import run_bass_kernel_spmd as _run

    nc = _bacc.Bacc("TRN2", target_bir_lowering=False, num_devices=1)
    arrays, args = {}, []
    for name in _INS:
        a = _np.ascontiguousarray(inputs[name])
        arrays[f"in_{name}_dram"] = a
        args.append(nc.dram_tensor(f"in_{name}_dram", a.shape, _mybir.dt.from_np(a.dtype), kind="ExternalInput").ap())
    inv_freq = _np.float32(10000.0) ** (-_np.arange(HD // 2, dtype=_np.float32) / _np.float32(HD // 2))
    theta = _np.arange(TOK, dtype=_np.float32)[:, None] * inv_freq[None, :]
    arrays["rope_dram"] = _np.stack([_np.cos(theta), _np.sin(theta)], axis=1).astype(_np.float32)
    args.append(nc.dram_tensor("rope_dram", (TOK, 2, HD // 2), _mybir.dt.float32, kind="ExternalInput").ap())
    args.append(nc.dram_tensor("out_0_dram", (1, TOK, D), _mybir.dt.float32, kind="ExternalOutput").ap())
    perceiver(nc, *args)
    r = _run(nc, [arrays], core_ids=[0])
    return r.results[0]["out_0_dram"]
```
